# Optimizing a Trainium2 kernel written in Bass

```python
import numpy as np
import jax
import jax.numpy as jnp

def _softmax(x, axis=-1):
    return jax.nn.softmax(x, axis=axis)

def _gelu(x):
    return jax.nn.gelu(x, approximate=True)

def _silu(x):
    return jax.nn.silu(x)

def _sigmoid(x):
    return jax.nn.sigmoid(x)

def _layernorm(x, axis=-1, eps=1e-05):
    m = jnp.mean(x, axis=axis, keepdims=True)
    v = jnp.var(x, axis=axis, keepdims=True)
    return (x - m) / jnp.sqrt(v + eps)

def _scatter_add(tgt, idx, src, axis=0):
    return tgt.at[idx].add(src)

def _segment_sum(src, seg, n):
    return jax.ops.segment_sum(src, seg, n)
kernel_name = 'mk_prb_d1_jaxref_r4_6a2564'

def setup_inputs(seed: int=0):
    np.random.seed(seed)
    _w = jnp.asarray

    def _L0_attn_setup():
        import jax, jax.numpy as jnp
        import numpy as np
        B, T, D = (2, 512, 256)
        H, W = (16, 64)
        HD = D // H
        key = jax.random.key(seed)
        ks = jax.random.split(key, 5)
        s = 0.02
        return {'x': jax.random.normal(ks[0], (B, T, D), dtype=jnp.float32), 'Wqkv': jax.random.normal(ks[1], (3 * D, D), dtype=jnp.float32) * s, 'bqkv': jax.random.normal(ks[2], (3 * D,), dtype=jnp.float32) * s, 'Wo': jax.random.normal(ks[3], (D, D), dtype=jnp.float32) * s, 'bo': jax.random.normal(ks[4], (D,), dtype=jnp.float32) * s}
    _L0_attn_in = _L0_attn_setup()

    def _L0_ffn_setup():
        import jax, jax.numpy as jnp
        import numpy as np
        DIM = 256
        HIDDEN = 768
        SCALE = 1.0 / 127.0

        def _dequant(w_int, dtype):
            return w_int.astype(dtype) * jnp.asarray(SCALE, dtype)
        key = jax.random.key(seed)
        k_x, k_g, k_u, k_d = jax.random.split(key, 4)
        x = jax.random.normal(k_x, (4, 512, DIM), dtype=jnp.float32)
        w_gate = jax.random.randint(k_g, (HIDDEN, DIM), -127, 128, dtype=jnp.int32)
        w_up = jax.random.randint(k_u, (HIDDEN, DIM), -127, 128, dtype=jnp.int32)
        w_down = jax.random.randint(k_d, (DIM, HIDDEN), -127, 128, dtype=jnp.int32)
        return {'x': x, 'w_gate': w_gate, 'w_up': w_up, 'w_down': w_down}
    _L0_ffn_in = _L0_ffn_setup()
    _d = {'L0_attn_x': _L0_attn_in['x'], 'L0_attn_Wqkv': _L0_attn_in['Wqkv'], 'L0_attn_bqkv': _L0_attn_in['bqkv'], 'L0_attn_Wo': _L0_attn_in['Wo'], 'L0_attn_bo': _L0_attn_in['bo'], 'L0_ffn_w_gate': _L0_ffn_in['w_gate'], 'L0_ffn_w_up': _L0_ffn_in['w_up'], 'L0_ffn_w_down': _L0_ffn_in['w_down']}
    _x0 = _d['L0_attn_x']
    _d['L0_attn_x'] = jax.random.normal(jax.random.fold_in(jax.random.key(seed), 1), (1, 4096, 256), dtype=_x0.dtype)
    del _x0
    return _d

def reference(L0_attn_x, L0_attn_Wqkv, L0_attn_bqkv, L0_attn_Wo, L0_attn_bo, L0_ffn_w_gate, L0_ffn_w_up, L0_ffn_w_down):

    def _L0_attn_ref(x, Wqkv, bqkv, Wo, bo):
        import jax, jax.numpy as jnp
        import numpy as np
        B, T, D = (2, 512, 256)
        H, W = (16, 64)
        HD = D // H
        b, t, d = x.shape
        qkv = x @ Wqkv.T + bqkv
        qkv = qkv.reshape(b, t, 3, H, HD)
        q = jnp.transpose(qkv[:, :, 0], (0, 2, 1, 3))
        k = jnp.transpose(qkv[:, :, 1], (0, 2, 1, 3))
        v = jnp.transpose(qkv[:, :, 2], (0, 2, 1, 3))
        scores = jnp.einsum('bhid,bhjd->bhij', q, k) / jnp.sqrt(jnp.float32(HD))
        i = jnp.arange(t)[:, None]
        j = jnp.arange(t)[None, :]
        mask = (j <= i) & (j >= i - (W - 1))
        scores = jnp.where(mask, scores, -jnp.inf)
        probs = jax.nn.softmax(scores, axis=-1)
        y = jnp.einsum('bhij,bhjd->bhid', probs, v)
        y = jnp.transpose(y, (0, 2, 1, 3)).reshape(b, t, d)
        return y @ Wo.T + bo

    def _L0_ffn_ref(x, w_gate, w_up, w_down):
        import jax, jax.numpy as jnp
        import numpy as np
        DIM = 256
        HIDDEN = 768
        SCALE = 1.0 / 127.0

        def _dequant(w_int, dtype):
            return w_int.astype(dtype) * jnp.asarray(SCALE, dtype)
        wg = _dequant(w_gate, x.dtype)
        wu = _dequant(w_up, x.dtype)
        wd = _dequant(w_down, x.dtype)
        gate = jnp.einsum('bsd,hd->bsh', x, wg)
        up = jnp.einsum('bsd,hd->bsh', x, wu)
        h = jax.nn.silu(gate) * up
        return jnp.einsum('bsh,dh->bsd', h, wd)
    x = L0_attn_x
    xn = _layernorm(x, axis=-1)
    x = x + _L0_attn_ref(xn, L0_attn_Wqkv, L0_attn_bqkv, L0_attn_Wo, L0_attn_bo) + _L0_ffn_ref(xn, L0_ffn_w_gate, L0_ffn_w_up, L0_ffn_w_down)
    return x

_drawn_inputs = setup_inputs


def setup_inputs(seed=0):
    import zlib

    import numpy as np

    out = dict(_drawn_inputs(seed))
    spreads = {}
    factors = {'L0_attn_Wqkv': 64.0, 'L0_attn_bqkv': 64.0, 'L0_attn_Wo': 64.0, 'L0_attn_bo': 64.0}
    for name, (base, spread) in spreads.items():
        noise = np.random.default_rng([zlib.crc32(name.encode()), seed]).standard_normal(out[name].shape)
        drawn = base * np.exp(spread * noise) if base else spread * noise
        out[name] = jnp.asarray(drawn.astype(out[name].dtype))
    for name, factor in factors.items():
        out[name] = (out[name] * factor).astype(out[name].dtype)
    return out
```

```python
from contextlib import ExitStack

import numpy as np

import concourse.bass as bass
from concourse import mybir

ALU = mybir.AluOpType
ACT = mybir.ActivationFunctionType
AX = mybir.AxisListType
F32 = mybir.dt.float32
F32R = mybir.dt.float32r
BF16 = mybir.dt.bfloat16
I32 = mybir.dt.int32

P = 128
T, D, HID = 4096, 256, 768
H, HD, W = 16, 16, 64
CH = 256
NC = T // CH
TPC = CH // P
KT = D // P
HT = HID // P
NQ = 4
QH = H // NQ
ROWS = 6 * HD + 1
VALID = 6 * HD
AUG = 112
SELR = W + 3 * H
NEG = -1.0e38
EPS = 1e-5
QSCALE = 1.0 / float(np.sqrt(HD))
WSCALE = 1.0 / 127.0
VW = HD + 1
PRODUCTS = ((0, 0), (0, 1), (1, 0), (1, 1), (0, 2), (2, 0))
WQKV, WO, WG = 0, KT * 6, KT * 6 + KT * 2
WU = WG + KT * HT
WD = WU + KT * HT
NBLK = WD + HT * 2


def head_of(g):
    return 8 * (g % 2) + g // 2


def window_mask():
    r, s = np.arange(W)[:, None], np.arange(2 * W)[None, :]
    outside = ((s < W) & (s <= r)) | ((s >= W) & (s - W > r))
    return np.where(outside, NEG, 0.0).astype(np.float32)


def shape_constants():
    bf = np.dtype("bfloat16")
    eye = np.eye(W, dtype=np.float32)
    mask = window_mask()
    sel = np.zeros((SELR, H, P), np.float32)
    sel[:W] = mask[:, None, :]
    for part in range(3):
        for g in range(H):
            sel[W + part * H + g, g, :] = 1.0
    left = np.zeros((P, W), np.float32)
    left[np.arange(P), np.arange(P) % W] = 1.0
    return {
        "ident": np.eye(P, dtype=np.float32),
        "identb": np.eye(P, dtype=np.float32).astype(bf),
        "pair": np.concatenate([eye, eye], 1).astype(bf),
        "mask4": np.tile(mask[:, None, :], (1, QH, 1)).astype(bf),
        "sel": sel.astype(bf),
        "left": left.astype(bf),
    }


def layer_program(nc, x, Wqkv, bqkv, Wo, bo, w_gate, w_up, w_down,
                  ident, identb, pair, mask4, sel, left, out):
    x_c = x.rearrange("a (c j p) d -> (a c) p j d", p=P, j=TPC)
    out_c = out.rearrange("a (c j p) d -> (a c) p j d", p=P, j=TPC)
    bq_cols = bqkv.rearrange("(m p) -> p m", p=P)
    bv_row = bqkv[2 * D:3 * D].rearrange("(a n) -> a n", a=1)
    bo_row = bo.rearrange("(a n) -> a n", a=1)
    scratch = nc.dram_tensor("qk_parts_dram", (2, 2, P, 3, 2, CH), BF16, kind="Internal").ap()

    with ExitStack() as ctx:
        def sb(name, shape, dt):
            return ctx.enter_context(nc.sbuf_tensor(name, shape, dt))

        def sem(name):
            return ctx.enter_context(nc.semaphore(name))

        def bank(name, dt=F32, n=512):
            return ctx.enter_context(nc.psum_tensor(name, [P, n], dt))

        ps_s = [bank(f"ps_s{i}") for i in range(2)]
        ps_t = [bank(f"ps_t{i}") for i in range(2)]
        ps_y = [bank(f"ps_y{i}") for i in range(2)]
        ps_d = [bank(f"ps_d{i}") for i in range(2)]

        identity = sb("identity", [P, P], F32)
        identity_b = sb("identity_b", [P, P], BF16)
        pair_eye = sb("pair_eye", [W, P], BF16)
        mask_quad = sb("mask_quad", [W, QH * P], BF16)
        mask_sel = sb("mask_sel", [SELR, H, P], BF16)
        minus_half = sb("minus_half", [P, TPC], F32)
        eps = sb("eps", [P, TPC], F32)
        one = sb("one", [P, H], F32)
        minus_one = sb("minus_one", [P, H], F32)
        bqk = sb("bqk", [P, 6], F32)
        bq_scaled = sb("bq_scaled", [P, 2], F32)
        bv = sb("bv", [P, D], F32)
        bo_rows = sb("bo_rows", [P, D], F32)
        w_hi = sb("w_hi", [P, NBLK, P], F32R)
        w_lo = sb("w_lo", [P, NBLK, P], F32R)
        raw_qkv = sb("raw_qkv", [P, 6, D], F32)
        raw_o = sb("raw_o", [P, 2, D], F32)
        raw_i = sb("raw_i", [P, 3, HT * D], I32)
        raw_f = raw_i[:].bitcast(F32)

        x_in = sb("x_in", [P, 2, TPC, D], F32)
        stats = sb("stats", [P, TPC, 6], F32)
        meanvar = sb("meanvar", [P, TPC, 2], F32)
        var_eps = sb("var_eps", [P, TPC], F32)
        rstd = sb("rstd", [P, TPC], F32)
        neg_mean = sb("neg_mean", [P, TPC], F32)
        shift = sb("shift", [P, TPC], F32)
        xn = sb("xn", [P, TPC, D], F32)
        xT_hi = sb("xT_hi", [P, 2, KT, CH], F32R)
        xT_lo = sb("xT_lo", [P, 2, KT, CH], F32R)
        x_bo = sb("x_bo", [P, 2, TPC, D], F32)
        qk_f = sb("qk_f", [P, 2, 2 * CH], F32)
        qk_parts = sb("qk_parts", [P, 2, 3, 2 * CH], BF16)
        v_f = sb("v_f", [P, TPC * D], F32)
        v_win = sb("v_win", [P, 2, TPC, 2, 2, H, VW], BF16)
        q_aug = [sb(f"q_aug{i}", [AUG, H // 2, 2, CH], BF16) for i in range(2)]
        k_aug = [sb(f"k_aug{i}", [AUG, H // 2, 2, W + CH], BF16) for i in range(2)]

        row_max = sb("row_max", [P, 2, H], F32)
        neg_max = sb("neg_max", [P, H], F32)
        neg_max_rest = sb("neg_max_rest", [P, H], F32)
        max_cols = sb("max_cols", [P, SELR], BF16)
        max_rows = sb("max_rows", [SELR, 2, P], BF16)
        p_f = sb("p_f", [P, 2, 512], F32)
        p_hi = sb("p_hi", [P, 2, 512], BF16)
        p_lo = sb("p_lo", [P, 2, 512], BF16)
        recip = sb("recip", [P, 2, QH * 2], F32)
        y = sb("y", [P, TPC, D], F32)
        tanh_g = sb("tanh_g", [P, 2, CH], F32)
        gate_t = sb("gate_t", [P, 2, CH], F32)
        h_f = sb("h_f", [P, 2, CH], F32)
        h_hi = sb("h_hi", [P, HT, CH], F32R)
        h_lo = sb("h_lo", [P, HT, CH], F32R)
        yT_hi = sb("yT_hi", [P, KT * CH], F32R)
        yT_lo = sb("yT_lo", [P, KT * CH], F32R)
        out_rows = sb("out_rows", [P, 2, TPC * D], F32)

        s_const = sem("s_const")
        s_raw = [sem(f"s_raw{i}") for i in range(5)]
        s_set = sem("s_set")
        s_bq = sem("s_bq")
        s_int = sem("s_int")
        s_wT = sem("s_wT")
        s_whi = sem("s_whi")
        s_wlo = sem("s_wlo")
        s_xin = [sem(f"s_xin{i}") for i in range(2)]
        s_stats = sem("s_stats")
        s_mv = sem("s_mv")
        s_ln = sem("s_ln")
        s_xn = sem("s_xn")
        s_xT = sem("s_xT")
        s_xhi = sem("s_xhi")
        s_xlo = sem("s_xlo")
        s_xbo = sem("s_xbo")
        s_proj = sem("s_proj")
        s_qkf = sem("s_qkf")
        s_qkhi = sem("s_qkhi")
        s_qkr = sem("s_qkr")
        s_qkmid = sem("s_qkmid")
        s_qklo = sem("s_qklo")
        s_vf = sem("s_vf")
        s_vhi = sem("s_vhi")
        s_vlo = sem("s_vlo")
        s_store = [sem(f"s_store{i}") for i in range(2)]
        s_qaug = sem("s_qaug")
        s_kaug = sem("s_kaug")
        s_vwin = sem("s_vwin")
        s_s = sem("s_s")
        s_max = sem("s_max")
        s_nm = sem("s_nm")
        s_mT = sem("s_mT")
        s_mrow = sem("s_mrow")
        s_t = sem("s_t")
        s_exp = sem("s_exp")
        s_phi = sem("s_phi")
        s_plo = sem("s_plo")
        s_pv = sem("s_pv")
        s_rec = sem("s_rec")
        s_y = sem("s_y")
        s_gu = sem("s_gu")
        s_tanh = sem("s_tanh")
        s_gt = sem("s_gt")
        s_hf = sem("s_hf")
        s_hhi = sem("s_hhi")
        s_hlo = sem("s_hlo")
        s_yT = sem("s_yT")
        s_yhi = sem("s_yhi")
        s_ylo = sem("s_ylo")
        s_out = sem("s_out")
        s_res = sem("s_res")
        s_done = [sem(f"s_done{i}") for i in range(2)]

        NCONST = 9
        NSET = 16
        QA, KA, VA = 16 * 6, 16 * 13, 16 * 3

        def wait(eng, s, count):
            if not isinstance(count, int) or count > 0:
                eng.wait_ge(s, count)

        def value(eng, count):
            if isinstance(count, int):
                return count
            register = eng.alloc_register(f"count{nc.next_id()}")
            eng.reg_mov(register, count)
            return eng.snap(register, min_val=0)

        def sweep(eng, step):
            step(0, 0)
            step(1, 1)
            with eng.Fori(1, NC // 2 - 1) as i:
                step(2 * i, 0)
                step(2 * i + 1, 1)
            step(NC - 2, 0)
            step(NC - 1, 1)

        def is_last(c, n=1):
            return isinstance(c, int) and c >= NC - n

        def is_first(c):
            return isinstance(c, int) and c == 0

        block = ctx.enter_context(nc.Block())

        @block.sync
        def _(sp):
            for i, (dst, src) in enumerate(((identity, ident), (identity_b, identb), (pair_eye, pair))):
                sp.dma_start(dst[:], src).then_inc(s_const, 16)
            sp.dma_start(x_in[:, 0], x_c[0]).then_inc(s_xin[0], 16)
            sp.dma_start(raw_qkv[:], Wqkv.rearrange("(o p) d -> p o d", p=P)).then_inc(s_raw[0], 16)
            sp.dma_start(raw_o[:], Wo.rearrange("(o p) d -> p o d", p=P)).then_inc(s_raw[1], 16)
            for n, w in enumerate((w_gate, w_up, w_down)):
                sp.dma_start(raw_i[:, n].rearrange("p (o d) -> p o d", d=w.shape[1]),
                             w.rearrange("(o p) d -> p o d", p=P)).then_inc(s_raw[2 + n], 16)
            sp.dma_start(mask_quad[:].rearrange("r (h s) -> r h s", h=QH), mask4).then_inc(s_const, 16)
            sp.dma_start(mask_sel[:], sel).then_inc(s_const, 16)
            sp.dma_start(max_cols[:, 0:W], left).then_inc(s_const, 16)
            with nc.allow_non_contiguous_dma(reason="biases, once"):
                sp.dma_start(bqk[:], bq_cols).then_inc(s_const, 16)
            sp.dma_start(bv[:], bv_row.partition_broadcast(P)).then_inc(s_const, 16)
            sp.dma_start(bo_rows[:], bo_row.partition_broadcast(P)).then_inc(s_const, 16)
            sp.dma_start(x_in[:, 1], x_c[1]).then_inc(s_xin[1], 16)

            def lay_out(c, b):
                prev = 1 - b
                c1, t1 = value(sp, c + 1), value(sp, 8 * (c - 1))
                vw, qa, ka = (value(sp, n * c - m) for n, m in ((VA, 0), (QA, 0), (KA, 16)))
                split1, split2, st = value(sp, 2 * c + 1), value(sp, 2 * c + 2), value(sp, 16 * (c + 1))
                wait(sp, s_pv, t1)
                sp.wait_ge(s_vhi, c1)
                sp.wait_ge(s_vlo, c1)
                wait(sp, s_vwin, vw)
                sp.dma_start(v_win[W:P, b, :, :, 0], v_win[0:W, b, :, :, 1]).then_inc(s_vwin, 16)
                sp.dma_start(v_win[0:W, b, 1, :, 0], v_win[W:P, b, 0, :, 1]).then_inc(s_vwin, 16)
                sp.dma_start(v_win[0:W, b, 0, :, 0], v_win[W:P, prev, 1, :, 1]).then_inc(s_vwin, 16)
                for which in range(2):
                    sp.wait_ge(s_qkmid, (split1, split2)[which])
                    sp.wait_ge(s_qklo, (split1, split2)[which])
                    wait(sp, (s_qaug, s_kaug)[which], (qa, ka)[which])
                    sp.dma_start(scratch[b, which].rearrange("p a m t -> p (a m t)"),
                                 qk_parts[:, which].rearrange("p a n -> p (a n)")).then_inc(s_store[which], 16)
                wait(sp, s_t, t1)
                if is_first(c):
                    sp.wait_ge(s_set, NSET)
                else:
                    sp.wait_ge(s_kaug, ka)
                    sp.dma_start(k_aug[b][:, :, :, 0:W], k_aug[prev][:, :, :, CH:CH + W]).then_inc(s_kaug, 16)
                for which in range(2):
                    sp.wait_ge(s_store[which], st)
                    for n, parts in enumerate(PRODUCTS):
                        rows = slice(HD * n, HD * n + HD)
                        src = scratch[b, which, :, parts[which]].rearrange("(h d) m t -> d h m t", d=HD)
                        if which == 0:
                            sp.dma_start(q_aug[b][rows].rearrange("d h m t -> d h (m t)"),
                                         src.rearrange("d h m t -> d h (m t)")).then_inc(s_qaug, 16)
                        else:
                            for m in range(2):
                                sp.dma_start(k_aug[b][rows, :, m, W:W + CH], src[:, :, m]).then_inc(s_kaug, 16)

            def step(c, b):
                c0, c1 = value(sp, c), value(sp, c + 1)
                if not is_last(c, 2):
                    sp.wait_ge(s_xbo, c1)
                    sp.wait_ge(s_xn, c1)
                    sp.dma_start(x_in[:, b], x_c[c + 2]).then_inc(s_xin[b], 16)
                if not is_last(c):
                    lay_out(c + 1, 1 - b)
                if not is_first(c):
                    sp.wait_ge(s_res, c0)
                    sp.dma_start(out_c[c - 1], out_rows[:, 1 - b].rearrange("p (j d) -> p j d", j=TPC)) \
                        .then_inc(s_done[1 - b], 16)

            lay_out(0, 0)
            sweep(sp, step)
            sp.wait_ge(s_res, NC)
            sp.dma_start(out_c[NC - 1], out_rows[:, 1].rearrange("p (j d) -> p j d", j=TPC)).then_inc(s_done[1], 16)
            sp.wait_ge(s_done[0], 16 * (NC // 2))
            sp.wait_ge(s_done[1], 16 * (NC // 2))

        @block.tensor
        def _(pe):
            def dense(dst, stat_hi, stat_lo, mov_hi, mov_lo, first, last):
                pe.matmul(dst, stat_hi, mov_hi, start=first, stop=False, skip_group_check=True)
                pe.matmul(dst, stat_lo, mov_hi, start=False, stop=False, skip_group_check=True)
                return pe.matmul(dst, stat_hi, mov_lo, start=False, stop=last, skip_group_check=True)

            def weights():
                blocks = [(raw_qkv[:, o, k * P:(k + 1) * P], 0) for k in range(KT) for o in range(6)]
                blocks += [(raw_o[:, o, k * P:(k + 1) * P], 1) for k in range(KT) for o in range(2)]
                for n in range(2):
                    src = raw_f[:, n].rearrange("p (o d) -> p o d", o=HT)
                    blocks += [(src[:, o, k * P:(k + 1) * P], 2 + n) for k in range(KT) for o in range(HT)]
                src = raw_f[:, 2].rearrange("p (o d) -> p o d", o=2)
                blocks += [(src[:, o, k * P:(k + 1) * P], 4) for k in range(HT) for o in range(2)]
                pe.wait_ge(s_const, 16 * NCONST)
                for n in range(NBLK // 4):
                    if n >= 2:
                        pe.wait_ge(s_wlo, n - 1)
                    for i in range(4):
                        src, come = blocks[4 * n + i]
                        if come < 2:
                            pe.wait_ge(s_raw[come], 16)
                        else:
                            pe.wait_ge(s_int, come - 1)
                        mm = pe.transpose(ps_d[n % 2][:, i * P:(i + 1) * P], src, identity[:])
                    mm.then_inc(s_wT, 1)

            def transpose_x(c):
                pe.wait_ge(s_xn, c + 1)
                for k in range(KT):
                    for j in range(TPC):
                        mm = pe.transpose(ps_d[0][:, k * CH + j * P:k * CH + (j + 1) * P],
                                          xn[:, j, k * P:(k + 1) * P], identity[:])
                mm.then_inc(s_xT, 1)

            def project(c, b, q_or_k):
                for m in range(2):
                    for k in range(KT):
                        blk = WQKV + k * 6 + 2 * q_or_k + m
                        mm = dense(ps_d[q_or_k][:, m * CH:(m + 1) * CH], w_hi[:, blk], w_lo[:, blk],
                                   xT_hi[:, b, k], xT_lo[:, b, k], k == 0, k == KT - 1)
                mm.then_inc(s_proj, 1)

            def project_v(c, b):
                for j in range(TPC):
                    for k in range(KT):
                        blk = WQKV + k * 6 + 4
                        tok = slice(j * P, (j + 1) * P)
                        mm = dense(ps_d[0][:, j * D:(j + 1) * D], xT_hi[:, b, k, tok], xT_lo[:, b, k, tok],
                                   w_hi[:, blk:blk + 2].rearrange("p a n -> p (a n)"),
                                   w_lo[:, blk:blk + 2].rearrange("p a n -> p (a n)"), k == 0, k == KT - 1)
                mm.then_inc(s_proj, 1)

            def transpose_y(c):
                pe.wait_ge(s_y, 4 * (c + 1))
                for k in range(KT):
                    for j in range(TPC):
                        mm = pe.transpose(ps_d[1][:, k * CH + j * P:k * CH + (j + 1) * P],
                                          y[:, j, k * P:(k + 1) * P], identity[:])
                mm.then_inc(s_yT, 1)

            def output(c):
                pe.wait_ge(s_yhi, c + 1)
                pe.wait_ge(s_ylo, c + 1)
                pe.wait_ge(s_hhi, HT * (c + 1))
                pe.wait_ge(s_hlo, HT * (c + 1))
                for j in range(TPC):
                    dst = ps_d[1][:, j * D:(j + 1) * D]
                    for k in range(KT):
                        tok = slice(k * CH + j * P, k * CH + (j + 1) * P)
                        blk = WO + k * 2
                        dense(dst, yT_hi[:, tok], yT_lo[:, tok],
                              w_hi[:, blk:blk + 2].rearrange("p a n -> p (a n)"),
                              w_lo[:, blk:blk + 2].rearrange("p a n -> p (a n)"), k == 0, False)
                    for k in range(HT):
                        blk = WD + k * 2
                        tok = slice(j * P, (j + 1) * P)
                        mm = dense(dst, h_hi[:, k, tok], h_lo[:, k, tok],
                                   w_hi[:, blk:blk + 2].rearrange("p a n -> p (a n)"),
                                   w_lo[:, blk:blk + 2].rearrange("p a n -> p (a n)"), False, k == HT - 1)
                mm.then_inc(s_out, 1)

            def gate_up(c, b, m):
                for n, first in enumerate((WG, WU)):
                    for k in range(KT):
                        blk = first + k * HT + m
                        mm = dense(ps_d[m % 2 if m < 3 else (m + 1) % 2][:, n * CH:(n + 1) * CH], w_hi[:, blk], w_lo[:, blk],
                                   xT_hi[:, b, k], xT_lo[:, b, k], k == 0, k == KT - 1)
                mm.then_inc(s_gu, 1)

            def scores_by_query(t, j, b, u):
                n = NQ * t + u
                wait(pe, s_max, n - 1)
                pe.matmul(ps_s[u % 2][:], pair_eye[:], mask_quad[:], start=True, stop=False, skip_group_check=True)
                for i in range(QH):
                    g = QH * u + i
                    for half in range(2):
                        tok = j * P + half * W
                        mm = pe.matmul(ps_s[u % 2][half * W:(half + 1) * W, i * P:(i + 1) * P],
                                       q_aug[b][0:ROWS, g // 2, g % 2, tok:tok + W],
                                       k_aug[b][0:ROWS, g // 2, g % 2, tok:tok + P],
                                       start=False, stop=(i == QH - 1), skip_group_check=True)
                mm.then_inc(s_s, 1)

            def transpose_max(t, j):
                pe.wait_ge(s_nm, 5 * (t + 1))
                pe.transpose(ps_d[1][:].bitcast(BF16)[0:SELR, 0:P], max_cols[:], identity_b[:]).then_inc(s_mT, 1)

            def scores_by_key(t, j, b, u):
                n = NQ * t + u
                wait(pe, s_exp, n - 1)
                for i in range(QH):
                    g = QH * u + i
                    pe.matmul(ps_t[u % 2][:, i * P:(i + 1) * P], mask_sel[:, g], max_rows[:, j],
                              start=True, stop=False, skip_group_check=True)
                    for half in range(2):
                        tok = j * P + half * W
                        mm = pe.matmul(ps_t[u % 2][:, i * P + half * W:i * P + (half + 1) * W],
                                       k_aug[b][0:ROWS, g // 2, g % 2, tok:tok + P],
                                       q_aug[b][0:ROWS, g // 2, g % 2, tok:tok + W],
                                       start=False, stop=True, skip_group_check=True)
                mm.then_inc(s_t, 1)

            def weighted_v(t, j, b, u):
                n = NQ * t + u
                pe.wait_ge(s_phi, n + 1)
                pe.wait_ge(s_plo, n + 1)
                wait(pe, s_y, 2 * t - 1 + u // 2)
                dst = ps_y[u // 2]
                for i in range(QH):
                    g = QH * u + i
                    col = (g % 8) * 2 * VW
                    o = dst[:, col:col + 2 * VW].rearrange("p (a v) -> p a v", a=2)
                    hi, lo = p_hi[:, u % 2, i * P:(i + 1) * P], p_lo[:, u % 2, i * P:(i + 1) * P]
                    v_hi, v_lo = v_win[:, b, j, 0, :, head_of(g)], v_win[:, b, j, 1, :, head_of(g)]
                    pe.matmul(o, hi, v_hi, start=True, stop=False, skip_group_check=True)
                    pe.matmul(o, hi, v_lo, start=False, stop=False, skip_group_check=True)
                    mm = pe.matmul(o, lo, v_hi, start=False, stop=True, skip_group_check=True)
                mm.then_inc(s_pv, 1)

            def step(c, b):
                nb = 1 - b
                if not is_last(c):
                    wait(pe, s_hf, HT * c)
                    transpose_x(c + 1)
                if not is_first(c):
                    pe.wait_ge(s_mrow, 2 * c + 1)
                    transpose_y(c - 1)
                if not is_last(c):
                    pe.wait_ge(s_xhi, c + 2)
                    pe.wait_ge(s_xlo, c + 2)
                    project(c + 1, nb, 0)
                    wait(pe, s_ylo, c)
                    if is_first(c):
                        pe.wait_ge(s_mrow, 1)
                    project(c + 1, nb, 1)
                    pe.wait_ge(s_qkf, 4 * c + 6)
                    project_v(c + 1, nb)
                    pe.wait_ge(s_qkf, 4 * c + 8)
                if not is_first(c):
                    output(c - 1)
                for j in range(TPC):
                    t = TPC * c + j
                    pe.wait_ge(s_mrow, t + 1)
                    ahead = not (is_last(c) and j == TPC - 1)
                    na, nbuf = (1, b) if j == 0 else (0, nb)
                    if j == 0:
                        pe.wait_ge(s_vwin, VA * (c + 1))
                    elif ahead:
                        pe.wait_ge(s_qaug, QA * (c + 2))
                        pe.wait_ge(s_kaug, KA * (c + 2) - 16)
                    for u in range(NQ):
                        if ahead:
                            scores_by_query(t + 1, na, nbuf, u)
                        scores_by_key(t, j, b, u)
                        if u < 3:
                            m = 3 * j + u
                            if m == 0 and not is_last(c):
                                pe.wait_ge(s_vf, c + 2)
                            elif m == 0:
                                pe.wait_ge(s_hf, HT * c)
                            elif m == 1:
                                wait(pe, s_res, c)
                            elif m == 4:
                                pe.wait_ge(s_mrow, 2 * c + 2)
                            else:
                                pe.wait_ge(s_hf, HT * c + (m - 1 if m != 3 else 3))
                            gate_up(c, b, m)
                        if u >= 1:
                            weighted_v(t, j, b, u - 1)
                    weighted_v(t, j, b, NQ - 1)
                    if ahead:
                        pe.wait_ge(s_hf, HT * c + (2 if j == 0 else 5))
                        transpose_max(t + 1, na)

            weights()
            pe.wait_ge(s_wlo, NBLK // 4)
            transpose_x(0)
            pe.wait_ge(s_xhi, 1)
            pe.wait_ge(s_xlo, 1)
            project(0, 0, 0)
            project(0, 0, 1)
            pe.wait_ge(s_qkf, 2)
            project_v(0, 0)
            pe.wait_ge(s_qaug, QA)
            pe.wait_ge(s_kaug, KA - 16)
            pe.wait_ge(s_set, NSET)
            for u in range(NQ):
                scores_by_query(0, 0, 0, u)
            pe.wait_ge(s_qkf, 4)
            transpose_max(0, 0)
            pe.wait_ge(s_vf, 1)
            sweep(pe, step)
            pe.wait_ge(s_hf, HT * NC)
            transpose_y(NC - 1)
            output(NC - 1)

        @block.scalar
        def _(act):
            def normalise(c, b):
                act.wait_ge(s_ln, 4 * (c + 1))
                wait(act, s_xT, c)
                for j in range(TPC):
                    ins = act.activation(xn[:, j], x_in[:, b, j], ACT.Identity, scale=rstd[:, j:j + 1], bias=shift[:, j:j + 1])
                ins.then_inc(s_xn, 1)

            def x_high(c, b):
                act.wait_ge(s_xT, c + 1)
                wait(act, s_gu, HT * (c - 1))
                act.activation(xT_hi[:, b].rearrange("p k t -> p (k t)"), ps_d[0][:], ACT.Copy).then_inc(s_xhi, 1)

            def qk_out(c):
                for which in range(2):
                    act.wait_ge(s_proj, 3 * c + which + 1)
                    wait(act, s_qklo, 2 * (c - 1) + which + 1)
                    for m in range(2):
                        bias = bq_scaled[:, m:m + 1] if which == 0 else bqk[:, 2 + m:3 + m]
                        act.activation(qk_f[:, which, m * CH:(m + 1) * CH], ps_d[which][:, m * CH:(m + 1) * CH],
                                       ACT.Identity, bias=bias, scale=(QSCALE, 1.0)[which]).then_inc(s_qkf, 1)

            def y_high(c):
                act.wait_ge(s_yT, c + 1)
                wait(act, s_out, c)
                act.activation(yT_hi[:], ps_d[1][:], ACT.Copy).then_inc(s_yhi, 1)

            def exponentials(t, u):
                n = NQ * t + u
                act.wait_ge(s_t, n + 1)
                wait(act, s_plo, n - 1)
                act.activation(p_f[:, u % 2], ps_t[u % 2][:], ACT.Exp).then_inc(s_exp, 1)
                act.wait_ge(s_exp, n + 1)
                wait(act, s_pv, n - 1)
                act.activation(p_hi[:, u % 2], p_f[:, u % 2], ACT.Copy).then_inc(s_phi, 1)

            def gate_tanh(c, m):
                act.wait_ge(s_gu, HT * c + m + 1)
                wait(act, s_gt, HT * c + m - 1)
                src = ps_d[m % 2 if m < 3 else (m + 1) % 2]
                act.activation(tanh_g[:, m % 2], src[:, 0:CH], ACT.Tanh, scale=0.5 * WSCALE).then_inc(s_tanh, 1)

            def h_high(c, m):
                act.wait_ge(s_hf, HT * c + m + 1)
                wait(act, s_out, c)
                act.activation(h_hi[:, m], h_f[:, m % 2], ACT.Copy).then_inc(s_hhi, 1)

            def max_out(t, j):
                act.wait_ge(s_mT, t + 1)
                wait(act, s_t, NQ * (t - 1))
                act.activation(max_rows[:, j], ps_d[1][:].bitcast(BF16)[0:SELR, 0:P], ACT.Copy).then_inc(s_mrow, 1)

            def step(c, b):
                if not is_last(c):
                    x_high(c + 1, 1 - b)
                if not is_first(c):
                    y_high(c - 1)
                if not is_last(c):
                    qk_out(c + 1)
                for j in range(TPC):
                    t = TPC * c + j
                    if j == 1 and not is_last(c, 2):
                        normalise(c + 2, b)
                    for u in range(NQ):
                        exponentials(t, u)
                        if u < 3:
                            gate_tanh(c, 3 * j + u)
                        if u >= 1:
                            h_high(c, 3 * j + u - 1)
                    if not (is_last(c) and j == 1):
                        max_out(t + 1, 1 - j)

            act.wait_ge(s_const, 16 * NCONST)
            act.activation(bq_scaled[:], bqk[:, 0:2], ACT.Copy, scale=QSCALE).then_inc(s_bq, 1)
            normalise(0, 0)
            for n in range(NBLK // 4):
                act.wait_ge(s_wT, n + 1)
                act.activation(w_hi[:, 4 * n:4 * n + 4].rearrange("p a n -> p (a n)"), ps_d[n % 2][:], ACT.Copy).then_inc(s_whi, 1)
            act.wait_ge(s_bq, 1)
            x_high(0, 0)
            qk_out(0)
            normalise(1, 1)
            max_out(0, 0)
            sweep(act, step)
            y_high(NC - 1)

        @block.vector
        def _(dve):
            def f32(ap):
                return ap.bitcast(F32)

            def moments(c, b):
                dve.wait_ge(s_xin[b], 16 * ((c - b) // 2 + 1) if isinstance(c, int) else 8 * (c - b) + 16)
                wait(dve, s_ln, 4 * c)
                for j in range(TPC):
                    ins = dve.bn_stats(stats[:, j], x_in[:, b, j])
                ins.then_inc(s_stats, 1)

            def mean_and_variance(c):
                for j in range(TPC):
                    ins = dve.bn_aggr(meanvar[:, j], stats[:, j])
                ins.then_inc(s_mv, 1)

            def x_low(c, b):
                dve.wait_ge(s_xhi, c + 1)
                dve.tensor_tensor(xT_lo[:, b].rearrange("p k t -> p (k t)"), ps_d[0][:],
                                  f32(xT_hi[:, b].rearrange("p k t -> p (k t)")), ALU.subtract).then_inc(s_xlo, 1)

            def qk_high(c):
                for which in range(2):
                    dve.wait_ge(s_qkf, 4 * c + 2 * which + 2)
                    wait(dve, s_store[which], 16 * c)
                    dve.tensor_copy(qk_parts[:, which, 0], qk_f[:, which]).then_inc(s_qkhi, 1)

            def qk_middle(c):
                for which in range(2):
                    dve.wait_ge(s_qkr, 2 * c + which + 1)
                    dve.tensor_copy(qk_parts[:, which, 1], qk_f[:, which]).then_inc(s_qkmid, 1)

            def v_high(c, b):
                dve.wait_ge(s_proj, 3 * c + 3)
                wait(dve, s_vlo, c)
                dve.tensor_tensor(v_f[:].rearrange("p (j n) -> p j n", j=TPC), ps_d[0][:].rearrange("p (j n) -> p j n", j=TPC),
                                  bv[:].rearrange("p (a n) -> p a n", a=1).to_broadcast([P, TPC, D]), ALU.add).then_inc(s_vf, 1)
                dve.wait_ge(s_vf, c + 1)
                wait(dve, s_pv, 8 * (c - 1))
                wait(dve, s_vwin, VA * c)
                dve.tensor_copy(v_win[:, b, :, 0, 1, :, 0:HD], v_f[:].rearrange("p (j h d) -> p j h d", j=TPC, h=H)).then_inc(s_vhi, 1)

            def y_low(c):
                dve.wait_ge(s_yhi, c + 1)
                dve.tensor_tensor(yT_lo[:], ps_d[1][:], f32(yT_hi[:]), ALU.subtract).then_inc(s_ylo, 1)

            def residual(c, b):
                dve.wait_ge(s_out, c + 1)
                dve.wait_ge(s_xbo, c + 1)
                wait(dve, s_done[b], 16 * ((c - b) // 2) if isinstance(c, int) else 8 * (c - b))
                dve.tensor_tensor(out_rows[:, b], ps_d[1][:], x_bo[:, b].rearrange("p j d -> p (j d)"), ALU.add).then_inc(s_res, 1)

            def maxima(t, j, u):
                n = NQ * t + u
                dve.wait_ge(s_s, n + 1)
                if u == 0:
                    wait(dve, s_nm, 5 * (t - 1))
                dve.tensor_reduce(row_max[:, j, QH * u:QH * u + QH], ps_s[u % 2][:].rearrange("p (h s) -> p h s", h=QH),
                                  AX.X, ALU.max).then_inc(s_max, 1)

            def p_low(t, u):
                n = NQ * t + u
                dve.wait_ge(s_phi, n + 1)
                dve.tensor_tensor(p_lo[:, u % 2], p_f[:, u % 2], p_hi[:, u % 2], ALU.subtract).then_inc(s_plo, 1)

            def hidden(c, m):
                dve.wait_ge(s_tanh, HT * c + m + 1)
                src = ps_d[m % 2 if m < 3 else (m + 1) % 2]
                dve.scalar_tensor_tensor(gate_t[:, m % 2], tanh_g[:, m % 2], 1.0, src[:, 0:CH], ALU.add, ALU.mult).then_inc(s_gt, 1)
                dve.wait_ge(s_gt, HT * c + m + 1)
                wait(dve, s_hhi, HT * c + m - 1)
                dve.scalar_tensor_tensor(h_f[:, m % 2], gate_t[:, m % 2], 0.5 * WSCALE ** 3, src[:, CH:2 * CH],
                                         ALU.mult, ALU.mult).then_inc(s_hf, 1)

            def h_low(c, m):
                dve.wait_ge(s_hhi, HT * c + m + 1)
                dve.tensor_tensor(h_lo[:, m], h_f[:, m % 2], f32(h_hi[:, m]), ALU.subtract).then_inc(s_hlo, 1)

            def normalise_y(c, t, j, n8):
                dve.wait_ge(s_pv, NQ * t + 2 * n8 + 2)
                if n8 == 0:
                    wait(dve, s_yT, c)
                v = ps_y[n8][:, 0:8 * 2 * VW].rearrange("p (h m a v) -> p h m a v", h=4, m=2, a=2)
                for half in range(2):
                    rows = slice(half * W, (half + 1) * W)
                    ins = dve.reciprocal(recip[rows, n8].rearrange("p (h m) -> p h m", m=2), v[rows, :, :, half, HD])
                ins.then_inc(s_rec, 1)
                dve.wait_ge(s_rec, 2 * t + n8 + 1)
                for half in range(2):
                    rows = slice(half * W, (half + 1) * W)
                    dst = y[rows, j].rearrange("p (m h d) -> p h m d", m=2, h=8)[:, 4 * n8:4 * n8 + 4]
                    r = recip[rows, n8].rearrange("p (h m a) -> p h m a", m=2, a=1).to_broadcast([W, 4, 2, HD])
                    ins = dve.tensor_tensor(dst, v[rows, :, :, half, 0:HD], r, ALU.mult)
                ins.then_inc(s_y, 1)

            def step(c, b):
                if not is_last(c):
                    x_low(c + 1, 1 - b)
                if not is_first(c):
                    y_low(c - 1)
                if not is_last(c):
                    qk_high(c + 1)
                    v_high(c + 1, 1 - b)
                    qk_middle(c + 1)
                if not is_first(c):
                    residual(c - 1, 1 - b)
                for j in range(TPC):
                    t = TPC * c + j
                    for u in range(NQ):
                        if not (is_last(c) and j == 1):
                            maxima(t + 1, 1 - j, u)
                        p_low(t, u)
                        if u < 3:
                            hidden(c, 3 * j + u)
                        if u >= 1:
                            h_low(c, 3 * j + u - 1)
                        if u == 3:
                            normalise_y(c, t, j, 0)
                    if j == 0 and not is_last(c, 2):
                        moments(c + 2, b)
                        dve.wait_ge(s_stats, c + 3)
                    normalise_y(c, t, j, 1)
                    if j == 0 and not is_last(c, 2):
                        mean_and_variance(c + 2)

            moments(0, 0)
            dve.wait_ge(s_stats, 1)
            mean_and_variance(0)
            for n in range(3):
                dve.wait_ge(s_raw[2 + n], 16)
                dve.tensor_copy(raw_f[:, n], raw_i[:, n]).then_inc(s_int, 1)
            for n in range(NBLK // 4):
                dve.wait_ge(s_whi, n + 1)
                span = slice(4 * n, 4 * n + 4)
                dve.tensor_tensor(w_lo[:, span].rearrange("p a n -> p (a n)"), ps_d[n % 2][:],
                                  f32(w_hi[:, span].rearrange("p a n -> p (a n)")), ALU.subtract).then_inc(s_wlo, 1)
            dve.wait_ge(s_const, 16 * NCONST)
            dve.wait_ge(s_set, NSET)
            x_low(0, 0)
            qk_high(0)
            v_high(0, 0)
            qk_middle(0)
            moments(1, 1)
            dve.wait_ge(s_stats, 2)
            mean_and_variance(1)
            for u in range(NQ):
                maxima(0, 0, u)
            sweep(dve, step)
            y_low(NC - 1)
            residual(NC - 1, 1)

        @block.gpsimd
        def _(pool):
            def scale_and_shift(c, b):
                pool.wait_ge(s_mv, c + 1)
                wait(pool, s_xn, c)
                pool.tensor_tensor(var_eps[:], meanvar[:, :, 1], eps[:], ALU.add).then_inc(s_ln, 1)
                pool.tensor_tensor(neg_mean[:], meanvar[:, :, 0], minus_one[:, 0:TPC], ALU.mult).then_inc(s_ln, 1)
                pool.wait_ge(s_ln, 4 * c + 2)
                pool.tensor_tensor(rstd[:], var_eps[:], minus_half[:], ALU.pow).then_inc(s_ln, 1)
                pool.wait_ge(s_ln, 4 * c + 3)
                pool.tensor_tensor(shift[:], neg_mean[:], rstd[:], ALU.mult).then_inc(s_ln, 1)

            def split(c, b):
                for which in range(2):
                    pool.wait_ge(s_qkhi, 2 * c + which + 1)
                    pool.tensor_tensor(qk_f[:, which], qk_f[:, which], qk_parts[:, which, 0], ALU.subtract).then_inc(s_qkr, 1)
                for which in range(2):
                    pool.wait_ge(s_qkmid, 2 * c + which + 1)
                    pool.tensor_tensor(qk_parts[:, which, 2], qk_f[:, which], qk_parts[:, which, 1], ALU.subtract).then_inc(s_qklo, 1)
                pool.wait_ge(s_vhi, c + 1)
                pool.tensor_tensor(v_win[:, b, :, 1, 1, :, 0:HD], v_f[:].rearrange("p (j h d) -> p j h d", j=TPC, h=H),
                                   v_win[:, b, :, 0, 1, :, 0:HD], ALU.subtract).then_inc(s_vlo, 1)

            def add_bo(c, b):
                pool.wait_ge(s_xin[b], 16 * ((c - b) // 2 + 1) if isinstance(c, int) else 8 * (c - b) + 16)
                wait(pool, s_res, c - 1)
                pool.tensor_tensor(x_bo[:, b], x_in[:, b],
                                   bo_rows[:].rearrange("p (a n) -> p a n", a=1).to_broadcast([P, TPC, D]), ALU.add).then_inc(s_xbo, 1)

            def max_parts(t, j):
                base = 5 * t
                pool.wait_ge(s_max, NQ * (t + 1))
                wait(pool, s_mT, t)
                parts = [max_cols[:, W + H * n:W + H * (n + 1)] for n in range(3)]
                pool.tensor_tensor(neg_max[:], row_max[:, j], minus_one[:], ALU.mult).then_inc(s_nm, 1)
                pool.tensor_tensor(parts[0], row_max[:, j], minus_one[:], ALU.mult).then_inc(s_nm, 1)
                pool.wait_ge(s_nm, base + 2)
                pool.tensor_tensor(neg_max_rest[:], neg_max[:], parts[0], ALU.subtract).then_inc(s_nm, 1)
                pool.wait_ge(s_nm, base + 3)
                pool.tensor_tensor(parts[1], neg_max_rest[:], one[:], ALU.mult).then_inc(s_nm, 1)
                pool.wait_ge(s_nm, base + 4)
                pool.tensor_tensor(parts[2], neg_max_rest[:], parts[1], ALU.subtract).then_inc(s_nm, 1)

            def step(c, b):
                if not is_last(c):
                    split(c + 1, 1 - b)
                    add_bo(c + 1, 1 - b)
                for j in range(TPC):
                    if not (is_last(c) and j == 1):
                        max_parts(TPC * c + j + 1, 1 - j)
                    if j == 0 and not is_last(c, 2):
                        scale_and_shift(c + 2, b)

            fills = [(one[:], 1.0), (minus_one[:], -1.0), (eps[:], EPS), (minus_half[:], -0.5)]
            fills += [(tile[:], 0.0) for tile in (*k_aug, *q_aug, v_win)]
            fills += [(k_aug[0][VALID:ROWS, :, :, 0:W], NEG), (q_aug[0][VALID:ROWS], 1.0), (q_aug[1][VALID:ROWS], 1.0)]
            fills += [(v_win[:, b, j, 0, :, :, HD:VW], 1.0) for b in range(2) for j in range(TPC)]
            for n, (tile, value_set) in enumerate(fills):
                wait(pool, s_set, n)
                pool.memset(tile, value_set).then_inc(s_set, 1)
            scale_and_shift(0, 0)
            pool.wait_ge(s_const, 16 * NCONST)
            split(0, 0)
            add_bo(0, 0)
            scale_and_shift(1, 1)
            max_parts(0, 0)
            sweep(pool, step)


_INS = ["L0_attn_x", "L0_attn_Wqkv", "L0_attn_bqkv", "L0_attn_Wo", "L0_attn_bo",
        "L0_ffn_w_gate", "L0_ffn_w_up", "L0_ffn_w_down"]


def kernel(**inputs):
    import concourse.bacc as bacc
    from concourse.bass_utils import run_bass_kernel_spmd

    nc = bacc.Bacc("TRN2", target_bir_lowering=False, num_devices=1)
    arrays, args = {}, []
    named = {name: np.ascontiguousarray(inputs[name]) for name in _INS} | shape_constants()
    for name, a in named.items():
        arrays[f"in_{name}"] = a
        args.append(nc.dram_tensor(f"in_{name}", a.shape, mybir.dt.from_np(a.dtype), kind="ExternalInput").ap())
    out = nc.dram_tensor("out_rows_dram", (1, T, D), F32, kind="ExternalOutput").ap()
    layer_program(nc, *args, out)
    r = run_bass_kernel_spmd(nc, [arrays], core_ids=[0])
    return r.results[0]["out_rows_dram"]
```

```python
from contextlib import ExitStack

import numpy as np

import concourse.bass as bass
from concourse import mybir

ALU = mybir.AluOpType
ACT = mybir.ActivationFunctionType
AX = mybir.AxisListType
F32 = mybir.dt.float32
F32R = mybir.dt.float32r
BF16 = mybir.dt.bfloat16
I32 = mybir.dt.int32

P = 128
T, D, HID = 4096, 256, 768
H, HD, W = 16, 16, 64
CH = 256
NC = T // CH
TPC = CH // P
KT = D // P
HT = HID // P
NQ = 4
QH = H // NQ
ROWS = 6 * HD + 1
VALID = 6 * HD
AUG = 112
SELR = W + 3 * H
NEG = -1.0e38
EPS = 1e-5
QSCALE = 1.0 / float(np.sqrt(HD))
WSCALE = 1.0 / 127.0
VW = HD + 1
PRODUCTS = ((0, 0), (0, 1), (0, 2), (1, 0), (1, 1), (2, 0))
GROUPS = ((0, 3, 0), (3, 2, 1), (5, 1, 2))
WQKV, WO, WG = 0, KT * 6, KT * 6 + KT * 2
WU = WG + KT * HT
WD = WU + KT * HT
NBLK = WD + HT * 2


def head_of(g):
    return 8 * (g % 2) + g // 2


def window_mask():
    r, s = np.arange(W)[:, None], np.arange(2 * W)[None, :]
    outside = ((s < W) & (s <= r)) | ((s >= W) & (s - W > r))
    return np.where(outside, NEG, 0.0).astype(np.float32)


def shape_constants():
    bf = np.dtype("bfloat16")
    eye = np.eye(W, dtype=np.float32)
    mask = window_mask()
    sel = np.zeros((SELR, H, P), np.float32)
    sel[:W] = mask[:, None, :]
    for part in range(3):
        for g in range(H):
            sel[W + part * H + g, g, :] = 1.0
    left = np.zeros((P, W), np.float32)
    left[np.arange(P), np.arange(P) % W] = 1.0
    return {
        "ident": np.eye(P, dtype=np.float32),
        "identb": np.eye(P, dtype=np.float32).astype(bf),
        "pair": np.concatenate([eye, eye], 1).astype(bf),
        "mask4": np.tile(mask[:, None, :], (1, QH, 1)).astype(bf),
        "sel": sel.astype(bf),
        "left": left.astype(bf),
    }


def layer_program(nc, x, Wqkv, bqkv, Wo, bo, w_gate, w_up, w_down,
                  ident, identb, pair, mask4, sel, left, out):
    x_c = x.rearrange("a (c j p) d -> (a c) p j d", p=P, j=TPC)
    out_c = out.rearrange("a (c j p) d -> (a c) p j d", p=P, j=TPC)
    bqk_rows = bqkv[0:2 * D].rearrange("(m p) -> m p", p=P)
    bv_row = bqkv[2 * D:3 * D].rearrange("(a n) -> a n", a=1)
    bo_row = bo.rearrange("(a n) -> a n", a=1)
    scratch = nc.dram_tensor("qk_parts_dram", (2, 2, 3, P, 2 * CH), BF16, kind="Internal").ap()

    with ExitStack() as ctx:
        def sb(name, shape, dt):
            return ctx.enter_context(nc.sbuf_tensor(name, shape, dt))

        def sem(name):
            return ctx.enter_context(nc.semaphore(name))

        def bank(name, dt=F32, n=512):
            return ctx.enter_context(nc.psum_tensor(name, [P, n], dt))

        ps_s = [bank(f"ps_s{i}") for i in range(2)]
        ps_t = [bank(f"ps_t{i}") for i in range(2)]
        ps_y = [bank(f"ps_y{i}") for i in range(2)]
        ps_d = [bank(f"ps_d{i}") for i in range(2)]

        identity = sb("identity", [P, P], F32)
        identity_b = sb("identity_b", [P, P], BF16)
        pair_eye = sb("pair_eye", [W, P], BF16)
        mask_quad = sb("mask_quad", [W, QH * P], BF16)
        mask_sel = sb("mask_sel", [SELR, H, P], BF16)
        minus_half = sb("minus_half", [P, TPC], F32)
        eps = sb("eps", [P, TPC], F32)
        one = sb("one", [P, H], F32)
        minus_one = sb("minus_one", [P, H], F32)
        bqk_in = sb("bqk_in", [4, P], F32)
        bqk_rows_dh = sb("bqk_rows_dh", [4, P], F32)
        bqk = sb("bqk", [P, 4], F32)
        bq_scaled = sb("bq_scaled", [P, 2], F32)
        bv = sb("bv", [P, D], F32)
        bo_rows = sb("bo_rows", [P, D], F32)
        w_hi = sb("w_hi", [P, NBLK, P], F32R)
        w_lo = sb("w_lo", [P, NBLK, P], F32R)
        raw_qkv = sb("raw_qkv", [P, 6, D], F32)
        raw_o = sb("raw_o", [P, 2, D], F32)
        raw_i = sb("raw_i", [P, 3, HT * D], I32)
        raw_f = raw_i[:].bitcast(F32)

        x_in = sb("x_in", [P, 2, TPC, D], F32)
        stats = sb("stats", [P, TPC, 6], F32)
        meanvar = sb("meanvar", [P, TPC, 2], F32)
        var_eps = sb("var_eps", [P, TPC], F32)
        rstd = sb("rstd", [P, TPC], F32)
        neg_mean = sb("neg_mean", [P, TPC], F32)
        shift = sb("shift", [P, TPC], F32)
        xn = sb("xn", [P, TPC, D], F32)
        xT_hi = sb("xT_hi", [P, 2, KT, CH], F32R)
        xT_lo = sb("xT_lo", [P, 2, KT, CH], F32R)
        x_bo = sb("x_bo", [P, 2, TPC, D], F32)
        qk_f = sb("qk_f", [P, 2, 2 * CH], F32)
        qk_parts = sb("qk_parts", [P, 2, 3, 2 * CH], BF16)
        v_f = sb("v_f", [P, TPC * D], F32)
        v_win = sb("v_win", [P, 2, TPC, 2, 2, H, VW], BF16)
        q_aug = [sb(f"q_aug{i}", [AUG, H // 2, 2, CH], BF16) for i in range(2)]
        k_aug = [sb(f"k_aug{i}", [AUG, H // 2, 2, W + CH], BF16) for i in range(2)]

        row_max = sb("row_max", [P, 2, H], F32)
        neg_max = sb("neg_max", [P, H], F32)
        neg_max_rest = sb("neg_max_rest", [P, H], F32)
        max_cols = sb("max_cols", [P, SELR], BF16)
        max_rows = sb("max_rows", [SELR, 2, P], BF16)
        p_f = raw_f[:, 0, 0:1024].rearrange("p (b n) -> p b n", b=2)
        p_hi = sb("p_hi", [P, 2, 512], BF16)
        p_lo = sb("p_lo", [P, 2, 512], BF16)
        recip = sb("recip", [P, 2, QH * 2], F32)
        y = sb("y", [P, TPC, D], F32)
        tanh_g = sb("tanh_g", [P, 2, CH], F32)
        h_f = sb("h_f", [P, 2, CH], F32)
        h_hi = sb("h_hi", [P, 2, HT, CH], F32R)
        h_lo = sb("h_lo", [P, 2, HT, CH], F32R)
        yT_hi = sb("yT_hi", [P, KT * CH], F32R)
        yT_lo = sb("yT_lo", [P, KT * CH], F32R)
        out_rows = sb("out_rows", [P, 2, TPC * D], F32)
        rest_sum = sb("rest_sum", [P, 1], F32)
        rest_squares = raw_f[:, 1:3].rearrange("p a n -> p (a n)").bitcast(BF16)[:, 0:(NBLK - WG) * P]
        ones_col = sb("ones_col", [P, 1], F32)
        rest_total = sb("rest_total", [1, 1], F32)

        first_fills = [(one[:], 1.0), (minus_one[:], -1.0), (eps[:], EPS), (minus_half[:], -0.5), (ones_col[:], 1.0)]
        def pairs(ap):
            return ap.bitcast(F32)

        two_ones = float(np.array([1.0, 1.0], np.dtype("bfloat16")).view(np.float32)[0])
        aug_fills = [(pairs(k_aug[b][VALID:AUG]), 0.0) for b in range(2)]
        aug_fills += [(pairs(q_aug[b][VALID:ROWS]), two_ones) for b in range(2)]
        aug_fills += [(pairs(k_aug[0][0:VALID, :, :, 0:W]), 0.0), (k_aug[0][VALID:ROWS, :, :, 0:W], NEG)]
        NAUG = len(aug_fills)
        fills = [(v_win[W:P, 1, 1, :, 1, :, 0:HD], 0.0)]
        fills += [(v_win[:, b, j, part, :, :, HD:VW], (1.0, 0.0)[part]) for part in range(2) for b in range(2) for j in range(TPC)]
        NSET = len(first_fills) + len(fills)

        s_ident = sem("s_ident")
        s_const = sem("s_const")
        s_raw = [sem(f"s_raw{i}") for i in range(5)]
        s_set = sem("s_set")
        s_augset = sem("s_augset")
        s_bqin = sem("s_bqin")
        s_bqr = sem("s_bqr")
        s_bqT = sem("s_bqT")
        s_bq = sem("s_bq")
        s_int = sem("s_int")
        s_wT = sem("s_wT")
        s_whi = sem("s_whi")
        s_wlo = sem("s_wlo")
        s_rest = sem("s_rest")
        s_restps = sem("s_restps")
        s_xin = [sem(f"s_xin{i}") for i in range(2)]
        s_stats = sem("s_stats")
        s_mv = sem("s_mv")
        s_ln = sem("s_ln")
        s_xn = sem("s_xn")
        s_xT = sem("s_xT")
        s_xhi = sem("s_xhi")
        s_xlo = sem("s_xlo")
        s_xbo = sem("s_xbo")
        s_proj = sem("s_proj")
        s_qkf = sem("s_qkf")
        s_qkhi = sem("s_qkhi")
        s_qkr = sem("s_qkr")
        s_qkmid = sem("s_qkmid")
        s_qklo = sem("s_qklo")
        s_vf = sem("s_vf")
        s_vhi = sem("s_vhi")
        s_vlo = sem("s_vlo")
        s_store = [sem(f"s_store{i}") for i in range(2)]
        s_qaug = sem("s_qaug")
        s_kaug = sem("s_kaug")
        s_vwin = sem("s_vwin")
        s_s = sem("s_s")
        s_max = sem("s_max")
        s_nm = sem("s_nm")
        s_mT = sem("s_mT")
        s_mrow = sem("s_mrow")
        s_t = sem("s_t")
        s_exp = sem("s_exp")
        s_phi = sem("s_phi")
        s_plo = sem("s_plo")
        s_pv = sem("s_pv")
        s_rec = sem("s_rec")
        s_y = sem("s_y")
        s_gu = sem("s_gu")
        s_tanh = sem("s_tanh")
        s_gt = sem("s_gt")
        s_hf = sem("s_hf")
        s_hhi = sem("s_hhi")
        s_hlo = sem("s_hlo")
        s_yT = sem("s_yT")
        s_yhi = sem("s_yhi")
        s_ylo = sem("s_ylo")
        s_out = sem("s_out")
        s_res = sem("s_res")
        s_done = [sem(f"s_done{i}") for i in range(2)]

        NCONST = 7
        QA, KA, VA = 16 * 3, 16 * 4, 16 * 3

        def wait(eng, s, count):
            if not isinstance(count, int) or count > 0:
                eng.wait_ge(s, count)

        def value(eng, count):
            if isinstance(count, int):
                return count
            register = eng.alloc_register(f"count{nc.next_id()}")
            eng.reg_mov(register, count)
            return eng.snap(register, min_val=0)

        def sweep(eng, step):
            step(0, 0)
            step(1, 1)
            with eng.Fori(1, NC // 2 - 1) as i:
                step(2 * i, 0)
                step(2 * i + 1, 1)
            step(NC - 2, 0)
            step(NC - 1, 1)

        def is_last(c, n=1):
            return isinstance(c, int) and c >= NC - n

        def is_first(c):
            return isinstance(c, int) and c == 0

        def hidden_bank(m):
            return 0 if m == 2 else 1

        def slot_ahead(c, b, k):
            n = k + NQ + 1
            tile = TPC * c + n // NQ
            j = n // NQ
            if isinstance(c, int) and tile >= TPC * NC:
                return None
            return tile, j % TPC, (b if j < TPC else 1 - b), n % NQ

        max_cols_T = ps_s[1][:].bitcast(BF16)[0:SELR, 0:P]

        block = ctx.enter_context(nc.Block())

        @block.sync
        def _(sp):
            sp.dma_start(x_in[:, 0], x_c[0]).then_inc(s_xin[0], 16)
            sp.dma_start(identity[:], ident).then_inc(s_ident, 16)
            sp.dma_start(raw_qkv[:], Wqkv.rearrange("(o p) d -> p o d", p=P)).then_inc(s_raw[0], 16)
            sp.dma_start(x_in[:, 1], x_c[1]).then_inc(s_xin[1], 16)
            sp.dma_start(bqk_in[:], bqk_rows).then_inc(s_bqin, 16)
            sp.dma_start(bv[:], bv_row.partition_broadcast(P)).then_inc(s_const, 16)
            sp.dma_start(bo_rows[:], bo_row.partition_broadcast(P)).then_inc(s_const, 16)
            sp.dma_start(identity_b[:], identb).then_inc(s_const, 16)
            sp.dma_start(pair_eye[:], pair).then_inc(s_const, 16)
            sp.dma_start(mask_quad[:].rearrange("r (h s) -> r h s", h=QH), mask4).then_inc(s_const, 16)
            sp.dma_start(mask_sel[:], sel).then_inc(s_const, 16)
            sp.dma_start(max_cols[:, 0:W], left).then_inc(s_const, 16)
            sp.dma_start(raw_o[:], Wo.rearrange("(o p) d -> p o d", p=P)).then_inc(s_raw[1], 16)
            for n, w in enumerate((w_gate, w_up, w_down)):
                sp.dma_start(raw_i[:, n].rearrange("p (o d) -> p o d", d=w.shape[1]),
                             w.rearrange("(o p) d -> p o d", p=P)).then_inc(s_raw[2 + n], 16)

            def lay_out_v(c, b):
                prev = 1 - b
                c1, t1, vw = value(sp, c + 1), value(sp, 8 * (c - 1)), value(sp, VA * c)
                wait(sp, s_pv, t1)
                sp.wait_ge(s_vhi, c1)
                sp.wait_ge(s_vlo, c1)
                wait(sp, s_vwin, vw)
                sp.dma_start(v_win[W:P, b, :, :, 0], v_win[0:W, b, :, :, 1]).then_inc(s_vwin, 16)
                sp.dma_start(v_win[0:W, b, 1, :, 0], v_win[W:P, b, 0, :, 1]).then_inc(s_vwin, 16)
                sp.dma_start(v_win[0:W, b, 0, :, 0], v_win[W:P, prev, 1, :, 1]).then_inc(s_vwin, 16)

            def store_parts(c, b, which):
                split, aug = value(sp, 2 * c + which + 1), value(sp, (QA * c, KA * c - 16)[which])
                sp.wait_ge(s_qkmid, split)
                sp.wait_ge(s_qklo, split)
                wait(sp, (s_qaug, s_kaug)[which], aug)
                sp.dma_start(scratch[b, which].rearrange("a p n -> p a n"), qk_parts[:, which]).then_inc(s_store[which], 16)

            def lay_out_qk(c, b):
                prev = 1 - b
                t1, st = value(sp, 8 * (c - 1)), value(sp, 16 * (c + 1))
                wait(sp, s_t, t1)
                if isinstance(c, int) and c < 2:
                    sp.wait_ge(s_augset, NAUG)
                if not is_first(c):
                    sp.dma_start(k_aug[b][:, :, :, 0:W], k_aug[prev][:, :, :, CH:CH + W]).then_inc(s_kaug, 16)
                for which in range(2):
                    sp.wait_ge(s_store[which], st)
                    for first, many, q_part in GROUPS:
                        rows = slice(HD * first, HD * (first + many))
                        if which == 0:
                            src = scratch[b, 0, q_part].rearrange("(a d h) n -> a d (h n)", a=1, d=HD).to_broadcast([many, HD, 8 * 2 * CH])
                            sp.dma_start(q_aug[b][rows].rearrange("r h m t -> r (h m t)"), src).then_inc(s_qaug, 16)
                        else:
                            src = scratch[b, 1, 0:many].rearrange("a (d h) (m t) -> (a d) (h m) t", d=HD, m=2)
                            sp.dma_start(k_aug[b][rows, :, :, W:W + CH].rearrange("r h m t -> r (h m) t"), src).then_inc(s_kaug, 16)

            def step(c, b):
                c0, c1 = value(sp, c), value(sp, c + 1)
                if not is_last(c, 2):
                    sp.wait_ge(s_xbo, c1)
                    sp.wait_ge(s_xn, c1)
                    sp.dma_start(x_in[:, b], x_c[c + 2]).then_inc(s_xin[b], 16)
                if not is_last(c):
                    store_parts(c + 1, 1 - b, 1)
                    lay_out_qk(c + 1, 1 - b)
                    lay_out_v(c + 1, 1 - b)
                if not is_first(c):
                    sp.wait_ge(s_res, c0)
                    sp.dma_start(out_c[c - 1], out_rows[:, 1 - b].rearrange("p (j d) -> p j d", j=TPC)) \
                        .then_inc(s_done[1 - b], 16)
                if not is_last(c, 2):
                    store_parts(c + 2, b, 0)

            for which in range(2):
                store_parts(0, 0, which)
            lay_out_qk(0, 0)
            sp.wait_ge(s_set, NSET)
            lay_out_v(0, 0)
            store_parts(1, 1, 0)
            sweep(sp, step)
            sp.wait_ge(s_res, NC)
            sp.dma_start(out_c[NC - 1], out_rows[:, 1].rearrange("p (j d) -> p j d", j=TPC)).then_inc(s_done[1], 16)
            sp.wait_ge(s_done[0], 16 * (NC // 2))
            sp.wait_ge(s_done[1], 16 * (NC // 2))

        @block.tensor
        def _(pe):
            def dense(dst, stat_hi, stat_lo, mov_hi, mov_lo, first, last):
                pairs = [(stat_hi, mov_hi), (stat_lo, mov_hi), (stat_hi, mov_lo)]
                pairs = [(a, m) for a, m in pairs if a is not None and m is not None]
                for n, (a, m) in enumerate(pairs):
                    mm = pe.matmul(dst, a, m, start=first and n == 0, stop=last and n == len(pairs) - 1,
                                   skip_group_check=True)
                return mm

            def weight_blocks():
                blocks = [(raw_qkv[:, o, k * P:(k + 1) * P], 0) for k in range(KT) for o in range(6)]
                blocks += [(raw_o[:, o, k * P:(k + 1) * P], 1) for k in range(KT) for o in range(2)]
                for n in range(2):
                    src = raw_f[:, n].rearrange("p (o d) -> p o d", o=HT)
                    blocks += [(src[:, o, k * P:(k + 1) * P], 2 + n) for k in range(KT) for o in range(HT)]
                src = raw_f[:, 2].rearrange("p (o d) -> p o d", o=2)
                blocks += [(src[:, o, k * P:(k + 1) * P], 4) for k in range(HT) for o in range(2)]
                return blocks

            blocks = weight_blocks()

            def transpose_weights(n):
                for i in range(4):
                    src, come = blocks[4 * n + i]
                    if come < 2:
                        pe.wait_ge(s_raw[come], 16)
                    else:
                        pe.wait_ge(s_int, come - 1)
                    dst = ps_d[n % 2][:, i * P:(i + 1) * P]
                    if 4 * n + i < 6 * KT and (4 * n + i) % 6 < 4:
                        dst = dst.rearrange("p (d h) -> p h d", d=HD)
                        src = src.rearrange("p (a n) -> p a n", a=1)
                    mm = pe.transpose(dst, src, identity[:])
                mm.then_inc(s_wT, 1)

            def transpose_x(c):
                pe.wait_ge(s_xn, c + 1)
                for k in range(KT):
                    for j in range(TPC):
                        mm = pe.transpose(ps_d[1][:, k * CH + j * P:k * CH + (j + 1) * P],
                                          xn[:, j, k * P:(k + 1) * P], identity[:])
                mm.then_inc(s_xT, 1)

            def project(c, b, q_or_k, bank=0):
                for m in range(2):
                    for k in range(KT):
                        blk = WQKV + k * 6 + 2 * q_or_k + m
                        mm = dense(ps_d[bank][:, m * CH:(m + 1) * CH], w_hi[:, blk], w_lo[:, blk],
                                   xT_hi[:, b, k], xT_lo[:, b, k], k == 0, k == KT - 1)
                mm.then_inc(s_proj, 1)

            def project_v(c, b):
                for j in range(TPC):
                    for k in range(KT):
                        blk = WQKV + k * 6 + 4
                        tok = slice(j * P, (j + 1) * P)
                        mm = dense(ps_d[0][:, j * D:(j + 1) * D], xT_hi[:, b, k, tok], xT_lo[:, b, k, tok],
                                   w_hi[:, blk:blk + 2].rearrange("p a n -> p (a n)"),
                                   w_lo[:, blk:blk + 2].rearrange("p a n -> p (a n)"), k == 0, k == KT - 1)
                mm.then_inc(s_proj, 1)

            def transpose_y(c):
                pe.wait_ge(s_y, 4 * (c + 1))
                for k in range(KT):
                    for j in range(TPC):
                        mm = pe.transpose(ps_d[0][:, k * CH + j * P:k * CH + (j + 1) * P],
                                          y[:, j, k * P:(k + 1) * P], identity[:])
                mm.then_inc(s_yT, 1)

            def output(c, b, j, exact):
                dst = ps_d[0][:, j * D:(j + 1) * D]
                for k in range(KT):
                    tok = slice(k * CH + j * P, k * CH + (j + 1) * P)
                    blk = WO + k * 2
                    dense(dst, yT_hi[:, tok], yT_lo[:, tok],
                          w_hi[:, blk:blk + 2].rearrange("p a n -> p (a n)"),
                          w_lo[:, blk:blk + 2].rearrange("p a n -> p (a n)"), k == 0, False)
                for k in range(HT):
                    blk = WD + k * 2
                    tok = slice(j * P, (j + 1) * P)
                    mm = dense(dst, h_hi[:, b, k, tok], h_lo[:, b, k, tok],
                               w_hi[:, blk:blk + 2].rearrange("p a n -> p (a n)"),
                               None if exact else w_lo[:, blk:blk + 2].rearrange("p a n -> p (a n)"),
                               False, k == HT - 1)
                if j == TPC - 1:
                    mm.then_inc(s_out, 1)

            def gate_up(c, b, m, exact):
                for n, first in enumerate((WG, WU)):
                    for k in range(KT):
                        blk = first + k * HT + m
                        mm = dense(ps_d[hidden_bank(m)][:, n * CH:(n + 1) * CH], w_hi[:, blk],
                                   None if exact else w_lo[:, blk], xT_hi[:, b, k], xT_lo[:, b, k],
                                   k == 0, k == KT - 1)
                mm.then_inc(s_gu, 1)

            def scores_by_query(t, j, b, u):
                n = NQ * t + u
                wait(pe, s_max, n - 1)
                pe.matmul(ps_s[u % 2][:], pair_eye[:], mask_quad[:], start=True, stop=False, skip_group_check=True)
                for i in range(QH):
                    g = QH * u + i
                    for half in range(2):
                        tok = j * P + half * W
                        mm = pe.matmul(ps_s[u % 2][half * W:(half + 1) * W, i * P:(i + 1) * P],
                                       q_aug[b][0:ROWS, g // 2, g % 2, tok:tok + W],
                                       k_aug[b][0:ROWS, g // 2, g % 2, tok:tok + P],
                                       start=False, stop=(i == QH - 1), skip_group_check=True)
                mm.then_inc(s_s, 1)

            def transpose_max(t):
                pe.wait_ge(s_nm, 5 * (t + 1))
                pe.transpose(max_cols_T, max_cols[:], identity_b[:]).then_inc(s_mT, 1)

            def scores_by_key(t, j, b, u):
                n = NQ * t + u
                wait(pe, s_exp, n - 1)
                for i in range(QH):
                    g = QH * u + i
                    pe.matmul(ps_t[u % 2][:, i * P:(i + 1) * P], mask_sel[:, g], max_rows[:, j],
                              start=True, stop=False, skip_group_check=True)
                    for half in range(2):
                        tok = j * P + half * W
                        mm = pe.matmul(ps_t[u % 2][:, i * P + half * W:i * P + (half + 1) * W],
                                       k_aug[b][0:ROWS, g // 2, g % 2, tok:tok + P],
                                       q_aug[b][0:ROWS, g // 2, g % 2, tok:tok + W],
                                       start=False, stop=True, skip_group_check=True)
                mm.then_inc(s_t, 1)

            def weighted_v(t, j, b, u):
                n = NQ * t + u
                pe.wait_ge(s_phi, n + 1)
                pe.wait_ge(s_plo, n + 1)
                wait(pe, s_y, 2 * t - 1 + u // 2)
                dst = ps_y[u // 2]
                for i in range(QH):
                    g = QH * u + i
                    col = (g % 8) * 2 * VW
                    o = dst[:, col:col + 2 * VW].rearrange("p (a v) -> p a v", a=2)
                    hi, lo = p_hi[:, u % 2, i * P:(i + 1) * P], p_lo[:, u % 2, i * P:(i + 1) * P]
                    v_hi, v_lo = v_win[:, b, j, 0, :, head_of(g)], v_win[:, b, j, 1, :, head_of(g)]
                    pe.matmul(o, hi, v_hi, start=True, stop=False, skip_group_check=True)
                    pe.matmul(o, hi, v_lo, start=False, stop=False, skip_group_check=True)
                    mm = pe.matmul(o, lo, v_hi, start=False, stop=True, skip_group_check=True)
                mm.then_inc(s_pv, 1)

            def fillers(c, b, k, exact):
                nb = 1 - b
                if k == 0:
                    if is_last(c):
                        pe.wait_ge(s_res, c - 1)
                    else:
                        pe.wait_ge(s_qkf, 4 * c + 8)
                    gate_up(c, b, 2, exact)
                    pe.wait_ge(s_hf, HT * c + 2)
                    gate_up(c, b, 3, exact)
                elif k == 1:
                    if not is_last(c):
                        pe.wait_ge(s_hf, HT * c + 3)
                        project_v(c + 1, nb)
                    pe.wait_ge(s_hf, HT * c + 4)
                    gate_up(c, b, 4, exact)
                elif k == 2:
                    if not is_first(c):
                        if not is_last(c):
                            pe.wait_ge(s_vf, c + 2)
                        transpose_y(c - 1)
                    pe.wait_ge(s_hf, HT * c + 5)
                    gate_up(c, b, 5, exact)
                elif k == 3:
                    if not is_first(c):
                        pe.wait_ge(s_yhi, c)
                        pe.wait_ge(s_ylo, c)
                        pe.wait_ge(s_hhi, HT * c)
                        pe.wait_ge(s_hlo, HT * c)
                        output(c - 1, nb, 0, exact)
                elif k == 4:
                    if not is_last(c, 2):
                        pe.wait_ge(s_hf, HT * c + 6)
                        transpose_x(c + 2)
                    if not is_first(c):
                        output(c - 1, nb, 1, exact)
                elif k == 5:
                    if not is_last(c, 2):
                        if is_first(c):
                            pe.wait_ge(s_vf, 2)
                        else:
                            pe.wait_ge(s_res, c)
                        pe.wait_ge(s_xhi, c + 3)
                        pe.wait_ge(s_xlo, c + 3)
                        project(c + 2, b, 0)
                    if not is_last(c):
                        pe.wait_ge(s_hf, HT * c + 6)
                        gate_up(c + 1, nb, 0, exact)
                elif k == 6:
                    if not is_last(c, 2):
                        pe.wait_ge(s_qkf, 4 * c + 10)
                        project(c + 2, b, 1)
                elif k == 7:
                    if not is_last(c):
                        pe.wait_ge(s_hf, HT * c + 7)
                        gate_up(c + 1, nb, 1, exact)

            def step(c, b, exact):
                for k in range(TPC * NQ):
                    j, u = k // NQ, k % NQ
                    t = TPC * c + j
                    ahead = slot_ahead(c, b, k)
                    if u == 0:
                        pe.wait_ge(s_mrow, t + 1)
                    if ahead is not None:
                        if k == NQ - 1:
                            pe.wait_ge(s_qaug, QA * (c + 2))
                            pe.wait_ge(s_kaug, KA * (c + 2) - 16)
                        scores_by_query(*ahead)
                    scores_by_key(t, j, b, u)
                    if u == NQ - 1 and not (is_last(c) and j == 1):
                        transpose_max(t + 1)
                    fillers(c, b, k, exact)
                    if k == 1:
                        pe.wait_ge(s_vwin, VA * (c + 1))
                    if k > 0:
                        before = k - 1
                        weighted_v(TPC * c + before // NQ, before // NQ, b, before % NQ)
                    elif not is_first(c):
                        weighted_v(t - 1, 1, 1 - b, NQ - 1)

            def all_steps(exact):
                gate_up(0, 0, 0, exact)
                pe.wait_ge(s_hf, 1)
                gate_up(0, 0, 1, exact)
                sweep(pe, lambda c, b: step(c, b, exact))
                weighted_v(2 * NC - 1, 1, 1, NQ - 1)
                pe.wait_ge(s_hf, HT * NC)
                transpose_y(NC - 1)
                pe.wait_ge(s_yhi, NC)
                pe.wait_ge(s_ylo, NC)
                pe.wait_ge(s_hhi, HT * NC)
                pe.wait_ge(s_hlo, HT * NC)
                for j in range(TPC):
                    output(NC - 1, 1, j, exact)

            pe.wait_ge(s_ident, 16)
            for n in range(3):
                if n == 2:
                    pe.wait_ge(s_wlo, 1)
                transpose_weights(n)
            pe.wait_ge(s_bqr, 1)
            pe.transpose(ps_t[1][:, 0:4], bqk_rows_dh[:], identity[0:4, 0:4]).then_inc(s_bqT, 1)
            pe.wait_ge(s_wlo, 2)
            transpose_x(0)
            pe.wait_ge(s_xhi, 1)
            pe.wait_ge(s_xlo, 1)
            pe.wait_ge(s_wlo, 3)
            project(0, 0, 0)
            project(0, 0, 1, bank=1)
            pe.wait_ge(s_qkf, 2)
            project_v(0, 0)
            pe.wait_ge(s_qkf, 4)
            transpose_weights(3)
            pe.wait_ge(s_wlo, 4)
            transpose_x(1)
            pe.wait_ge(s_vf, 1)
            pe.wait_ge(s_xhi, 2)
            pe.wait_ge(s_xlo, 2)
            project(1, 1, 0)
            project(1, 1, 1, bank=1)
            for n in range(4, NBLK // 4):
                if n == 4:
                    pe.wait_ge(s_qkf, 6)
                elif n == 5:
                    pe.wait_ge(s_qkf, 8)
                pe.wait_ge(s_wlo, n - 1)
                transpose_weights(n)
            pe.wait_ge(s_const, 16 * NCONST)
            pe.wait_ge(s_qaug, QA)
            pe.wait_ge(s_kaug, KA - 16)
            pe.wait_ge(s_augset, NAUG)
            for u in range(NQ):
                scores_by_query(0, 0, 0, u)
            scores_by_query(1, 1, 0, 0)
            pe.wait_ge(s_wlo, NBLK // 4)
            pe.wait_ge(s_set, len(first_fills))
            pe.wait_ge(s_rest, 1)
            pe.matmul(ps_t[0][0:1, 0:1], rest_sum[:], ones_col[:], start=True, stop=True).then_inc(s_restps, 1)
            transpose_max(0)
            pe.wait_ge(s_rest, 2)
            rest = pe.alloc_register("rest")
            pe.reg_load(rest, rest_total[:].bitcast(I32))
            with pe.If_eq(rest, 0):
                all_steps(True)
            with pe.Else():
                all_steps(False)

        @block.scalar
        def _(act):
            def f32(ap):
                return ap.bitcast(F32)

            def normalise(c, b):
                act.wait_ge(s_ln, 4 * (c + 1))
                wait(act, s_xT, c)
                for j in range(TPC):
                    ins = act.activation(xn[:, j], x_in[:, b, j], ACT.Identity, scale=rstd[:, j:j + 1], bias=shift[:, j:j + 1])
                ins.then_inc(s_xn, 1)

            def x_high(c, b):
                act.wait_ge(s_xT, c + 1)
                wait(act, s_gu, HT * (c - 1))
                act.activation(xT_hi[:, b].rearrange("p k t -> p (k t)"), ps_d[1][:], ACT.Copy).then_inc(s_xhi, 1)

            def qk_out(c, which, bank=0):
                act.wait_ge(s_proj, 3 * c + which + 1)
                wait(act, s_qklo, 2 * (c - 1) + which + 1)
                for m in range(2):
                    bias = bq_scaled[:, m:m + 1] if which == 0 else bqk[:, 2 + m:3 + m]
                    act.activation(qk_f[:, which, m * CH:(m + 1) * CH], ps_d[bank][:, m * CH:(m + 1) * CH],
                                   ACT.Identity, bias=bias, scale=(QSCALE, 1.0)[which]).then_inc(s_qkf, 1)

            def y_high(c):
                act.wait_ge(s_yT, c + 1)
                wait(act, s_out, c)
                act.activation(yT_hi[:], ps_d[0][:], ACT.Copy).then_inc(s_yhi, 1)

            def exponentials(t, u):
                n = NQ * t + u
                act.wait_ge(s_t, n + 1)
                wait(act, s_plo, n - 1)
                act.activation(p_f[:, u % 2], ps_t[u % 2][:], ACT.Exp).then_inc(s_exp, 1)

            def p_high(t, u):
                n = NQ * t + u
                act.wait_ge(s_exp, n + 1)
                wait(act, s_pv, n - 1)
                act.activation(p_hi[:, u % 2], p_f[:, u % 2], ACT.Copy).then_inc(s_phi, 1)

            def gate_tanh(c, m):
                act.wait_ge(s_gu, HT * c + m + 1)
                wait(act, s_gt, HT * c + m - 1)
                src = ps_d[hidden_bank(m)]
                act.activation(tanh_g[:, m % 2], src[:, 0:CH], ACT.Tanh, scale=0.5 * WSCALE).then_inc(s_tanh, 1)

            def h_high(c, b, m):
                act.wait_ge(s_hf, HT * c + m + 1)
                wait(act, s_out, c - 1)
                act.activation(h_hi[:, b, m], h_f[:, m % 2], ACT.Copy).then_inc(s_hhi, 1)

            def max_out(t, j):
                act.wait_ge(s_mT, t + 1)
                wait(act, s_t, NQ * (t - 1))
                act.activation(max_rows[:, j], max_cols_T, ACT.Copy).then_inc(s_mrow, 1)

            def step(c, b):
                nb = 1 - b
                for k in range(TPC * NQ):
                    j, u = k // NQ, k % NQ
                    t = TPC * c + j
                    if k < 4:
                        for m in ((1,), (2, 3), (4,), (5,))[k]:
                            h_high(c, b, m)
                    elif k == 6 and not is_last(c):
                        h_high(c + 1, nb, 0)
                    exponentials(t, u)
                    if u == NQ - 1 and not (is_last(c) and j == 1):
                        max_out(t + 1, 1 - j)
                    if k == 4 and not is_last(c, 2):
                        x_high(c + 2, b)
                    if k == 2 and not is_first(c):
                        y_high(c - 1)
                    p_high(t, u)
                    if k == 0:
                        gate_tanh(c, 2)
                        gate_tanh(c, 3)
                    elif k == 1:
                        gate_tanh(c, 4)
                    elif k == 2:
                        gate_tanh(c, 5)
                    elif k == 3 and not is_last(c, 2):
                        normalise(c + 2, b)
                    elif k == 5:
                        if not is_last(c, 2):
                            qk_out(c + 2, 0)
                        if not is_last(c):
                            gate_tanh(c + 1, 0)
                    elif k == 6 and not is_last(c, 2):
                        qk_out(c + 2, 1)
                    elif k == 7 and not is_last(c):
                        gate_tanh(c + 1, 1)

            def weights_high(n):
                act.wait_ge(s_wT, n + 1)
                act.activation(w_hi[:, 4 * n:4 * n + 4].rearrange("p a n -> p (a n)"), ps_d[n % 2][:],
                               ACT.Copy).then_inc(s_whi, 1)

            normalise(0, 0)
            act.wait_ge(s_bqin, 16)
            act.activation(bqk_rows_dh[:].rearrange("m (d h) -> m d h", d=HD), bqk_in[:].rearrange("m (h d) -> m d h", d=HD),
                           ACT.Copy).then_inc(s_bqr, 1)
            for n in range(3):
                weights_high(n)
            x_high(0, 0)
            act.wait_ge(s_bqT, 1)
            act.activation(bqk[:], ps_t[1][:, 0:4], ACT.Copy).then_inc(s_bq, 1)
            act.activation(bq_scaled[:], ps_t[1][:, 0:2], ACT.Copy, scale=QSCALE).then_inc(s_bq, 1)
            act.wait_ge(s_bq, 2)
            qk_out(0, 0)
            qk_out(0, 1, bank=1)
            weights_high(3)
            normalise(1, 1)
            x_high(1, 1)
            qk_out(1, 0)
            qk_out(1, 1, bank=1)
            for n in range(4, NBLK // 4):
                weights_high(n)
            act.wait_ge(s_wlo, NBLK // 4)
            act.activation(rest_squares, f32(w_lo[:, WG:NBLK].rearrange("p a n -> p (a n)")), ACT.Square,
                           accum_out=rest_sum[:]).then_inc(s_rest, 1)
            max_out(0, 0)
            gate_tanh(0, 0)
            h_high(0, 0, 0)
            gate_tanh(0, 1)
            sweep(act, step)
            y_high(NC - 1)

        @block.vector
        def _(dve):
            def f32(ap):
                return ap.bitcast(F32)

            def moments(c, b):
                dve.wait_ge(s_xin[b], 16 * ((c - b) // 2 + 1) if isinstance(c, int) else 8 * (c - b) + 16)
                wait(dve, s_ln, 4 * c)
                for j in range(TPC):
                    ins = dve.bn_stats(stats[:, j], x_in[:, b, j])
                ins.then_inc(s_stats, 1)

            def mean_and_variance(c):
                for j in range(TPC):
                    ins = dve.bn_aggr(meanvar[:, j], stats[:, j])
                ins.then_inc(s_mv, 1)

            def x_low(c, b):
                dve.wait_ge(s_xhi, c + 1)
                dve.tensor_tensor(xT_lo[:, b].rearrange("p k t -> p (k t)"), ps_d[1][:],
                                  f32(xT_hi[:, b].rearrange("p k t -> p (k t)")), ALU.subtract).then_inc(s_xlo, 1)

            def qk_high(c, which):
                dve.wait_ge(s_qkf, 4 * c + 2 * which + 2)
                wait(dve, s_store[which], 16 * c)
                dve.tensor_copy(qk_parts[:, which, 0], qk_f[:, which]).then_inc(s_qkhi, 1)

            def qk_middle(c, which):
                dve.wait_ge(s_qkr, 2 * c + which + 1)
                dve.tensor_copy(qk_parts[:, which, 1], qk_f[:, which]).then_inc(s_qkmid, 1)

            def v_high(c, b):
                dve.wait_ge(s_proj, 3 * c + 3)
                if is_first(c):
                    dve.wait_ge(s_const, 16 * NCONST)
                wait(dve, s_vlo, c)
                dve.tensor_tensor(v_f[:].rearrange("p (j n) -> p j n", j=TPC), ps_d[0][:].rearrange("p (j n) -> p j n", j=TPC),
                                  bv[:].rearrange("p (a n) -> p a n", a=1).to_broadcast([P, TPC, D]), ALU.add).then_inc(s_vf, 1)
                dve.wait_ge(s_vf, c + 1)
                wait(dve, s_pv, 8 * (c - 1))
                wait(dve, s_vwin, VA * c)
                dve.tensor_copy(v_win[:, b, :, 0, 1, :, 0:HD], v_f[:].rearrange("p (j h d) -> p j h d", j=TPC, h=H)).then_inc(s_vhi, 1)

            def y_low(c):
                dve.wait_ge(s_yhi, c + 1)
                dve.tensor_tensor(yT_lo[:], ps_d[0][:], f32(yT_hi[:]), ALU.subtract).then_inc(s_ylo, 1)

            def residual(c, b):
                dve.wait_ge(s_out, c + 1)
                dve.wait_ge(s_xbo, c + 1)
                wait(dve, s_done[b], 16 * ((c - b) // 2) if isinstance(c, int) else 8 * (c - b))
                dve.tensor_tensor(out_rows[:, b], ps_d[0][:], x_bo[:, b].rearrange("p j d -> p (j d)"), ALU.add).then_inc(s_res, 1)

            def maxima(t, j, u):
                n = NQ * t + u
                dve.wait_ge(s_s, n + 1)
                if u == 0:
                    wait(dve, s_nm, 5 * (t - 1))
                dve.tensor_reduce(row_max[:, j, QH * u:QH * u + QH], ps_s[u % 2][:].rearrange("p (h s) -> p h s", h=QH),
                                  AX.X, ALU.max).then_inc(s_max, 1)

            def p_low(t, u):
                n = NQ * t + u
                dve.wait_ge(s_phi, n + 1)
                dve.tensor_tensor(p_lo[:, u % 2], p_f[:, u % 2], p_hi[:, u % 2], ALU.subtract).then_inc(s_plo, 1)

            def hidden(c, m):
                dve.wait_ge(s_tanh, HT * c + m + 1)
                src = ps_d[hidden_bank(m)]
                dve.scalar_tensor_tensor(tanh_g[:, m % 2], tanh_g[:, m % 2], 1.0, src[:, 0:CH], ALU.add, ALU.mult).then_inc(s_gt, 1)
                dve.wait_ge(s_gt, HT * c + m + 1)
                wait(dve, s_hhi, HT * c + m - 1)
                dve.scalar_tensor_tensor(h_f[:, m % 2], tanh_g[:, m % 2], 0.5 * WSCALE ** 3, src[:, CH:2 * CH],
                                         ALU.mult, ALU.mult).then_inc(s_hf, 1)

            def h_low(c, b, m):
                dve.wait_ge(s_hhi, HT * c + m + 1)
                dve.tensor_tensor(h_lo[:, b, m], h_f[:, m % 2], f32(h_hi[:, b, m]), ALU.subtract).then_inc(s_hlo, 1)

            def normalise_y(c, t, j, n8):
                dve.wait_ge(s_pv, NQ * t + 2 * n8 + 2)
                if n8 == 0 and j == 0:
                    wait(dve, s_yT, c)
                v = ps_y[n8][:, 0:8 * 2 * VW].rearrange("p (h m a v) -> p h m a v", h=4, m=2, a=2)
                for half in range(2):
                    rows = slice(half * W, (half + 1) * W)
                    ins = dve.reciprocal(recip[rows, n8].rearrange("p (h m) -> p h m", m=2), v[rows, :, :, half, HD])
                ins.then_inc(s_rec, 1)
                dve.wait_ge(s_rec, 2 * t + n8 + 1)
                for half in range(2):
                    rows = slice(half * W, (half + 1) * W)
                    dst = y[rows, j].rearrange("p (m h d) -> p h m d", m=2, h=8)[:, 4 * n8:4 * n8 + 4]
                    r = recip[rows, n8].rearrange("p (h m a) -> p h m a", m=2, a=1).to_broadcast([W, 4, 2, HD])
                    ins = dve.tensor_tensor(dst, v[rows, :, :, half, 0:HD], r, ALU.mult)
                ins.then_inc(s_y, 1)

            def step(c, b):
                nb = 1 - b
                for k in range(TPC * NQ):
                    j, u = k // NQ, k % NQ
                    t = TPC * c + j
                    ahead = slot_ahead(c, b, k)
                    if ahead is not None:
                        maxima(ahead[0], ahead[1], ahead[3])
                    if k == 1 and not is_first(c):
                        normalise_y(c - 1, t - 1, 1, 1)
                    elif k in (3, 7):
                        normalise_y(c, t, j, 0)
                    elif k == 5:
                        normalise_y(c, t - 1, 0, 1)
                    if k < 4:
                        for m in ((1,), (2, 3), (4,), (5,))[k]:
                            h_low(c, b, m)
                    elif k == 6 and not is_last(c):
                        h_low(c + 1, nb, 0)
                    if k == 6 and not is_last(c, 2):
                        qk_middle(c + 2, 0)
                    elif k == 7 and not is_last(c, 2):
                        qk_high(c + 2, 1)
                    p_low(t, u)
                    if k == 0:
                        hidden(c, 2)
                        hidden(c, 3)
                    elif k == 1:
                        if not is_last(c):
                            v_high(c + 1, nb)
                        hidden(c, 4)
                        if not is_last(c, 2):
                            moments(c + 2, b)
                    elif k == 2:
                        if not is_first(c):
                            y_low(c - 1)
                        if not is_last(c, 2):
                            dve.wait_ge(s_stats, c + 3)
                        hidden(c, 5)
                        if not is_last(c, 2):
                            mean_and_variance(c + 2)
                    elif k == 4:
                        if not is_last(c, 2):
                            x_low(c + 2, b)
                        if not is_first(c):
                            residual(c - 1, nb)
                    elif k == 5:
                        if not is_last(c, 2):
                            qk_high(c + 2, 0)
                        if not is_last(c):
                            hidden(c + 1, 0)
                    elif k == 7:
                        if not is_last(c, 2):
                            qk_middle(c + 2, 1)
                        if not is_last(c):
                            hidden(c + 1, 1)

            def weights_low(n):
                dve.wait_ge(s_whi, n + 1)
                span = slice(4 * n, 4 * n + 4)
                dve.tensor_tensor(w_lo[:, span].rearrange("p a n -> p (a n)"), ps_d[n % 2][:],
                                  f32(w_hi[:, span].rearrange("p a n -> p (a n)")), ALU.subtract).then_inc(s_wlo, 1)

            moments(0, 0)
            dve.wait_ge(s_stats, 1)
            mean_and_variance(0)
            for n in range(3):
                weights_low(n)
            x_low(0, 0)
            qk_high(0, 0)
            moments(1, 1)
            qk_high(0, 1)
            qk_middle(0, 0)
            dve.wait_ge(s_stats, 2)
            qk_middle(0, 1)
            mean_and_variance(1)
            weights_low(3)
            dve.wait_ge(s_set, NSET)
            v_high(0, 0)
            x_low(1, 1)
            for which in range(2):
                qk_high(1, which)
            for which in range(2):
                qk_middle(1, which)
            for n in range(3):
                dve.wait_ge(s_raw[2 + n], 16)
                dve.tensor_copy(raw_f[:, n], raw_i[:, n]).then_inc(s_int, 1)
            for n in range(4, NBLK // 4):
                weights_low(n)
            for u in range(NQ):
                maxima(0, 0, u)
            maxima(1, 1, 0)
            dve.wait_ge(s_restps, 1)
            dve.tensor_copy(rest_total[:], ps_t[0][0:1, 0:1]).then_inc(s_rest, 1)
            hidden(0, 0)
            h_low(0, 0, 0)
            hidden(0, 1)
            sweep(dve, step)
            normalise_y(NC - 1, 2 * NC - 1, 1, 1)
            y_low(NC - 1)
            residual(NC - 1, 1)

        @block.gpsimd
        def _(pool):
            def scale_and_shift(c, b):
                pool.wait_ge(s_mv, c + 1)
                wait(pool, s_xn, c)
                pool.tensor_tensor(var_eps[:], meanvar[:, :, 1], eps[:], ALU.add).then_inc(s_ln, 1)
                pool.tensor_tensor(neg_mean[:], meanvar[:, :, 0], minus_one[:, 0:TPC], ALU.mult).then_inc(s_ln, 1)
                pool.wait_ge(s_ln, 4 * c + 2)
                pool.tensor_tensor(rstd[:], var_eps[:], minus_half[:], ALU.pow).then_inc(s_ln, 1)
                pool.wait_ge(s_ln, 4 * c + 3)
                pool.tensor_tensor(shift[:], neg_mean[:], rstd[:], ALU.mult).then_inc(s_ln, 1)

            def qk_rest(c, which):
                pool.wait_ge(s_qkhi, 2 * c + which + 1)
                pool.tensor_tensor(qk_f[:, which], qk_f[:, which], qk_parts[:, which, 0], ALU.subtract).then_inc(s_qkr, 1)

            def qk_low(c, which):
                pool.wait_ge(s_qkmid, 2 * c + which + 1)
                pool.tensor_tensor(qk_parts[:, which, 2], qk_f[:, which], qk_parts[:, which, 1], ALU.subtract).then_inc(s_qklo, 1)

            def v_low(c, b):
                pool.wait_ge(s_vhi, c + 1)
                pool.tensor_tensor(v_win[:, b, :, 1, 1, :, 0:HD], v_f[:].rearrange("p (j h d) -> p j h d", j=TPC, h=H),
                                   v_win[:, b, :, 0, 1, :, 0:HD], ALU.subtract).then_inc(s_vlo, 1)

            def add_bo(c, b):
                pool.wait_ge(s_xin[b], 16 * ((c - b) // 2 + 1) if isinstance(c, int) else 8 * (c - b) + 16)
                wait(pool, s_res, c - 1)
                pool.tensor_tensor(x_bo[:, b], x_in[:, b],
                                   bo_rows[:].rearrange("p (a n) -> p a n", a=1).to_broadcast([P, TPC, D]), ALU.add).then_inc(s_xbo, 1)

            def max_parts(t, j):
                base = 5 * t
                pool.wait_ge(s_max, NQ * (t + 1))
                wait(pool, s_mT, t)
                parts = [max_cols[:, W + H * n:W + H * (n + 1)] for n in range(3)]
                pool.tensor_tensor(neg_max[:], row_max[:, j], minus_one[:], ALU.mult).then_inc(s_nm, 1)
                pool.tensor_tensor(parts[0], row_max[:, j], minus_one[:], ALU.mult).then_inc(s_nm, 1)
                pool.wait_ge(s_nm, base + 2)
                pool.tensor_tensor(neg_max_rest[:], neg_max[:], parts[0], ALU.subtract).then_inc(s_nm, 1)
                pool.wait_ge(s_nm, base + 3)
                pool.tensor_tensor(parts[1], neg_max_rest[:], one[:], ALU.mult).then_inc(s_nm, 1)
                pool.wait_ge(s_nm, base + 4)
                pool.tensor_tensor(parts[2], neg_max_rest[:], parts[1], ALU.subtract).then_inc(s_nm, 1)

            def step(c, b):
                if not is_last(c):
                    v_low(c + 1, 1 - b)
                max_parts(TPC * c + 1, 1)
                if not is_last(c, 2):
                    scale_and_shift(c + 2, b)
                if not is_last(c):
                    add_bo(c + 1, 1 - b)
                if not is_last(c, 2):
                    qk_rest(c + 2, 0)
                if not is_last(c):
                    max_parts(TPC * c + 2, 0)
                if not is_last(c, 2):
                    qk_low(c + 2, 0)
                    qk_rest(c + 2, 1)
                    qk_low(c + 2, 1)

            def fill(n, tile, first_value):
                wait(pool, s_set, n)
                pool.memset(tile, first_value).then_inc(s_set, 1)

            for n, (tile, first_value) in enumerate(first_fills):
                fill(n, tile, first_value)
            pool.wait_ge(s_set, len(first_fills))
            scale_and_shift(0, 0)
            pool.wait_ge(s_ln, 4)
            for n, (tile, first_value) in enumerate(fills):
                fill(len(first_fills) + n, tile, first_value)
            pool.wait_ge(s_set, NSET)
            for n, (tile, first_value) in enumerate(aug_fills[0:4]):
                wait(pool, s_augset, n)
                pool.memset(tile, first_value).then_inc(s_augset, 1)
            pool.wait_ge(s_augset, 4)
            qk_rest(0, 0)
            qk_rest(0, 1)
            qk_low(0, 0)
            qk_low(0, 1)
            scale_and_shift(1, 1)
            v_low(0, 0)
            pool.wait_ge(s_vlo, 1)
            for n, (tile, first_value) in enumerate(aug_fills[4:]):
                pool.wait_ge(s_augset, 4 + n)
                pool.memset(tile, first_value).then_inc(s_augset, 1)
            pool.wait_ge(s_augset, NAUG)
            qk_rest(1, 0)
            qk_rest(1, 1)
            qk_low(1, 0)
            qk_low(1, 1)
            pool.wait_ge(s_const, 16 * NCONST)
            add_bo(0, 0)
            max_parts(0, 0)
            sweep(pool, step)


_INS = ["L0_attn_x", "L0_attn_Wqkv", "L0_attn_bqkv", "L0_attn_Wo", "L0_attn_bo",
        "L0_ffn_w_gate", "L0_ffn_w_up", "L0_ffn_w_down"]


def kernel(**inputs):
    import concourse.bacc as bacc
    from concourse.bass_utils import run_bass_kernel_spmd

    nc = bacc.Bacc("TRN2", target_bir_lowering=False, num_devices=1)
    arrays, args = {}, []
    named = {name: np.ascontiguousarray(inputs[name]) for name in _INS} | shape_constants()
    for name, a in named.items():
        arrays[f"in_{name}"] = a
        args.append(nc.dram_tensor(f"in_{name}", a.shape, mybir.dt.from_np(a.dtype), kind="ExternalInput").ap())
    out = nc.dram_tensor("out_rows_dram", (1, T, D), F32, kind="ExternalOutput").ap()
    layer_program(nc, *args, out)
    r = run_bass_kernel_spmd(nc, [arrays], core_ids=[0])
    return r.results[0]["out_rows_dram"]
```
